# Optimizing a Trainium2 kernel written in Bass

```python
import numpy as np
import jax
import jax.numpy as jnp

def _softmax(x, axis=-1):
    return jax.nn.softmax(x, axis=axis)

def _gelu(x):
    return jax.nn.gelu(x, approximate=True)

def _silu(x):
    return jax.nn.silu(x)

def _sigmoid(x):
    return jax.nn.sigmoid(x)

def _layernorm(x, axis=-1, eps=1e-05):
    m = jnp.mean(x, axis=axis, keepdims=True)
    v = jnp.var(x, axis=axis, keepdims=True)
    return (x - m) / jnp.sqrt(v + eps)

def _scatter_add(tgt, idx, src, axis=0):
    return tgt.at[idx].add(src)

def _segment_sum(src, seg, n):
    return jax.ops.segment_sum(src, seg, n)
kernel_name = 'mk_gnn_preln_d2_gnn_r8_527622'

def setup_inputs(seed: int=0):
    np.random.seed(seed)
    _w = jnp.asarray

    def _rec_inputs():
        import jax
        import jax.numpy as jnp
        _gk = jax.random.key(seed)
        x = -0.000202 + 1 * jax.random.normal(jax.random.fold_in(_gk, 1), (12500, 64), jnp.float32)
        _s = jax.random.randint(jax.random.fold_in(_gk, 2), (200000,), 0, 12500, jnp.int32)
        _d = jax.random.randint(jax.random.fold_in(_gk, 3), (200000,), 0, 12500, jnp.int32)
        _loop = jnp.arange(12500, dtype=jnp.int32)
        src = jnp.concatenate([_s, _d, _loop])
        dst = jnp.concatenate([_d, _s, _loop])
        _o = jnp.argsort(dst, stable=True)
        src = src[_o]
        dst = dst[_o]
        edge_attr_64 = 0.000189758 + 1.00013 * jax.random.normal(jax.random.fold_in(_gk, 12), (412500, 64), jnp.float32)
        return (x, src, dst, edge_attr_64)
    x, src, dst, edge_attr_64 = _rec_inputs()

    def _L0_gnn_setup():
        import jax, jax.numpy as jnp
        import numpy as np
        N_NODES = 12500
        N_EDGES = 156250
        D_FEAT = 64

        def _aggregate(x, src, dst, num_nodes):
            return jax.ops.segment_sum(x[src], dst, num_segments=num_nodes)
        key = jax.random.key(seed)
        kx, ke = jax.random.split(key)
        x = jax.random.normal(kx, (N_NODES, D_FEAT), dtype=jnp.float32)
        edge_index = jax.random.randint(ke, (2, N_EDGES), 0, N_NODES, dtype=jnp.int64)
        return {'x': x, 'edge_index': edge_index}
    _L0_gnn_all = _L0_gnn_setup()
    _L0_gnn_in = {k: v for k, v in _L0_gnn_all.items() if k in ()}
    del _L0_gnn_all

    def _L1_gnn_setup():
        import jax, jax.numpy as jnp
        import numpy as np
        N_NODES = 6250
        N_EDGES = 100000
        D = 64

        def _mlp(h, w1, b1, w2, b2):
            h = jax.nn.relu(h @ w1 + b1)
            return h @ w2 + b2
        key = jax.random.key(seed)
        ks = jax.random.split(key, 12)

        def lin(k, fan_in, fan_out):
            bound = 1.0 / np.sqrt(fan_in)
            kw, kb = jax.random.split(k)
            w = jax.random.uniform(kw, (fan_in, fan_out), jnp.float32, -bound, bound)
            b = jax.random.uniform(kb, (fan_out,), jnp.float32, -bound, bound)
            return (w, b)
        x = jax.random.normal(ks[0], (N_NODES, D), jnp.float32)
        edge_index = jax.random.randint(ks[1], (2, N_EDGES), 0, N_NODES, jnp.int64 if jax.config.jax_enable_x64 else jnp.int32)
        edge_attr = jax.random.normal(ks[2], (N_EDGES, D), jnp.float32)
        u = jax.random.normal(ks[3], (1, D), jnp.float32)
        batch = jnp.zeros((N_NODES,), dtype=edge_index.dtype)
        w1a, b1a = lin(ks[4], 2 * D, D)
        w1b, b1b = lin(ks[5], D, D)
        w2a, b2a = lin(ks[6], 2 * D, D)
        w2b, b2b = lin(ks[7], D, D)
        return dict(x=x, edge_index=edge_index, edge_attr=edge_attr, u=u, batch=batch, w1a=w1a, b1a=b1a, w1b=w1b, b1b=b1b, w2a=w2a, b2a=b2a, w2b=w2b, b2b=b2b)
    _L1_gnn_all = _L1_gnn_setup()
    _L1_gnn_in = {k: v for k, v in _L1_gnn_all.items() if k in ('u', 'w1a', 'b1a', 'w1b', 'b1b', 'w2a', 'b2a', 'w2b', 'b2b')}
    del _L1_gnn_all
    return {'x': x, 'src': src, 'dst': dst, 'edge_attr_64': edge_attr_64, 'L1_gnn_u': _L1_gnn_in['u'], 'L1_gnn_w1a': _L1_gnn_in['w1a'], 'L1_gnn_b1a': _L1_gnn_in['b1a'], 'L1_gnn_w1b': _L1_gnn_in['w1b'], 'L1_gnn_b1b': _L1_gnn_in['b1b'], 'L1_gnn_w2a': _L1_gnn_in['w2a'], 'L1_gnn_b2a': _L1_gnn_in['b2a'], 'L1_gnn_w2b': _L1_gnn_in['w2b'], 'L1_gnn_b2b': _L1_gnn_in['b2b']}

def reference(x, src, dst, edge_attr_64, L1_gnn_u, L1_gnn_w1a, L1_gnn_b1a, L1_gnn_w1b, L1_gnn_b1b, L1_gnn_w2a, L1_gnn_b2a, L1_gnn_w2b, L1_gnn_b2b):
    import jax
    import jax.numpy as jnp

    def _L0_gnn_ref(x, edge_index):
        import jax, jax.numpy as jnp
        import numpy as np
        N_NODES = 12500
        N_EDGES = 156250
        D_FEAT = 64

        def _aggregate(x, src, dst, num_nodes):
            return jax.ops.segment_sum(x[src], dst, num_segments=num_nodes)
        num_nodes = x.shape[0]
        src, dst = (edge_index[0], edge_index[1])
        h = _aggregate(x, src, dst, num_nodes)
        h = jax.nn.relu(h)
        h = _aggregate(h, src, dst, num_nodes)
        return h

    def _L1_gnn_ref(x, edge_index, edge_attr, u, batch, w1a, b1a, w1b, b1b, w2a, b2a, w2b, b2b):
        import jax, jax.numpy as jnp
        import numpy as np
        N_NODES = 6250
        N_EDGES = 100000
        D = 64

        def _mlp(h, w1, b1, w2, b2):
            h = jax.nn.relu(h @ w1 + b1)
            return h @ w2 + b2
        row, col = (edge_index[0], edge_index[1])
        n = x.shape[0]
        h = jnp.concatenate([x[row], edge_attr], axis=1)
        h = _mlp(h, w1a, b1a, w1b, b1b)
        summed = jax.ops.segment_sum(h, col, num_segments=n)
        counts = jax.ops.segment_sum(jnp.ones((h.shape[0],), h.dtype), col, num_segments=n)
        agg = summed / jnp.maximum(counts, 1.0)[:, None]
        out = jnp.concatenate([x, agg], axis=1)
        return _mlp(out, w2a, b2a, w2b, b2b)
    edge_index = jnp.stack([src, dst])
    batch0 = jnp.zeros((12500,), jnp.int32)
    h = jnp.maximum(_layernorm(x, axis=-1), 0.0)
    x = x + _L0_gnn_ref(h, edge_index)
    h = jnp.maximum(_layernorm(x, axis=-1), 0.0)
    x = x + _L1_gnn_ref(h, edge_index, edge_attr_64, L1_gnn_u, batch0, L1_gnn_w1a, L1_gnn_b1a, L1_gnn_w1b, L1_gnn_b1b, L1_gnn_w2a, L1_gnn_b2a, L1_gnn_w2b, L1_gnn_b2b)
    return x

_drawn_inputs = setup_inputs


def setup_inputs(seed=0):
    import zlib

    import numpy as np

    out = dict(_drawn_inputs(seed))
    spreads = {}
    factors = {'edge_attr_64': 8.0,
     'L1_gnn_w1a': 8.0,
     'L1_gnn_b1a': 32.462,
     'L1_gnn_w1b': 8.0,
     'L1_gnn_b1b': 47.537,
     'L1_gnn_w2a': 8.0,
     'L1_gnn_b2a': 184.214,
     'L1_gnn_w2b': 8.0,
     'L1_gnn_b2b': 200.0}
    for name, (base, spread) in spreads.items():
        noise = np.random.default_rng([zlib.crc32(name.encode()), seed]).standard_normal(out[name].shape)
        drawn = base * np.exp(spread * noise) if base else spread * noise
        out[name] = jnp.asarray(drawn.astype(out[name].dtype))
    for name, factor in factors.items():
        out[name] = (out[name] * factor).astype(out[name].dtype)
    return out
```

```python
from contextlib import ExitStack

import concourse.bass as bass
from concourse import mybir

P = 128
TILE = 128
TILES = 8
RING = 4
WINDOW = 64
CHUNK = 7
EPS = 1e-5

ALU = mybir.AluOpType
ACT = mybir.ActivationFunctionType
F32 = mybir.dt.float32
I32 = mybir.dt.int32
I16 = mybir.dt.int16
U32 = mybir.dt.uint32
AX = mybir.AxisListType
RMAX = bass.bass_isa.ReduceOp.max


def gnn_kernel(nc, x, src, dst, attr, w1a, b1a, w1b, b1b, w2a, b2a, w2b, b2b, out):
    n_nodes, D = out.shape
    NT = x.shape[0] // P
    NCH = NT // CHUNK
    NG = attr.shape[0]
    CW = CHUNK * P
    RW = CHUNK * D
    BANK = 512
    COLS = NT * P + WINDOW
    GROUP_LANDED = 16 * TILES
    SHIFT = WINDOW.bit_length() - 1
    FULL = n_nodes // P
    REST = n_nodes - FULL * P
    assert NCH * CHUNK == NT and NCH % 2 == 0 and TILES * D <= BANK and RW <= BANK and CW <= 2 * BANK
    assert n_nodes < NT * P and WINDOW == 1 << SHIFT and NG % RING and TILE == P

    with ExitStack() as ctx:
        def sb(name, shape, dt=F32):
            return ctx.enter_context(nc.sbuf_tensor(name, shape, dt))

        def sem(name):
            return ctx.enter_context(nc.semaphore(name))

        tables = [nc.dram_tensor(f"table{k}", [NT * P, D], F32).ap() for k in range(3)]
        psum = ctx.enter_context(nc.psum_tensor("psum", [P, 8 * BANK], F32))

        def bank(b, width=BANK):
            return psum[:, b * BANK:b * BANK + width]

        src_all = sb("src_all", [P, NG + RING, TILES], I32)
        dst_rel = sb("dst_rel", [P, NG, TILES])
        plan = sb("plan", [P, NG, 4], I32)
        node_no = sb("node_no", [P, COLS], I16)
        staged = sb("staged", [P, RING, TILES], U32)
        ring = sb("ring", [P, RING, TILES, D])
        attr_ring = sb("attr_ring", [P, RING, TILES // 2 * TILE])
        hit = sb("hit", [P, TILES, WINDOW])
        pre = sb("pre", [P, 2, TILES * D])
        msg = sb("msg", [P, 2, TILES, D + 1])
        tick = sb("tick", [P, 1])

        x_rows = sb("x_rows", [P, NT, D])
        rows = sb("rows", [P, NT, D])
        arena = sb("arena", [P, COLS])
        col_a = sb("col_a", [P, NT])
        col_b = sb("col_b", [P, NT])
        stage_t = sb("stage_t", [D, 2, CW])
        stage_r = sb("stage_r", [P, 2, RW])
        h_t = sb("h_t", [D, CW])
        inv_count = stage_t[:, 0, :]
        mean_t = stage_t[:, 1, :]
        hid_t = sb("hid_t", [D + 1, CW])

        sums = arena[0:D + 1, :]
        work = arena[:, 0:NT * D]
        table_rows = arena[:, NT * D:2 * NT * D]
        at_ = [NT * D]

        def scratch(n):
            at_[0] += n
            return arena[:, at_[0] - n:at_[0]]

        dst_i = scratch(NG * TILES).bitcast(I32)
        span = scratch(2 * NG)
        span_all = scratch(2 * NG)
        windows_i = scratch(NG).bitcast(I32)
        windows = scratch(NG)
        visits = scratch(NG)
        assert at_[0] <= COLS
        last, minus_first = span_all[:, 0:NG], span_all[:, NG:2 * NG]

        ident = sb("ident", [P, P])
        eps = sb("eps", [P, 1])
        w_attr = sb("w_attr", [P, 2 * D])
        w_node = sb("w_node", [D, D])
        b1a_all = sb("b1a_all", [P, D])
        w1b_b = sb("w1b_b", [D + 1, D])
        count_all = sb("count_all", [D + 1, D])
        w2a_h = sb("w2a_h", [D, D])
        w2a_m = sb("w2a_m", [D, D])
        b2a_col = sb("b2a_col", [D, 1])
        w2b_b = sb("w2b_b", [D + 1, D])

        dst_loaded = sem("dst_loaded")
        x_loaded = sem("x_loaded")
        src_loaded = sem("src_loaded")
        weights_loaded = sem("weights_loaded")
        pool_consts = sem("pool_consts")
        consts = sem("consts")
        plan_step = sem("plan_step")
        spans_reduced = sem("spans_reduced")
        plan_ready = sem("plan_ready")
        norm_step = [sem(f"norm_step{k}") for k in range(2)]
        std_ready = [sem(f"std_ready{k}") for k in range(2)]
        table_stored = [sem(f"table_stored{k}") for k in range(3)]
        indices_staged = [sem(f"indices_staged{k}") for k in range(3)]
        gathered = [[sem(f"gathered{k}_{r}") for r in range(RING)] for k in range(3)]
        slot_free = [sem(f"slot_free{k}") for k in range(3)]
        hit_built = [sem(f"hit_built{k}") for k in range(3)]
        scattered = [sem(f"scattered{k}") for k in range(3)]
        summed = [sem(f"summed{k}") for k in range(3)]
        attr_loaded = [sem(f"attr_loaded{r}") for r in range(RING)]
        multiplied = sem("multiplied")
        msg_ready = sem("msg_ready")
        msg_used = sem("msg_used")
        sums_staged = [sem(f"sums_staged{k}") for k in range(2)]
        sums_turned = [sem(f"sums_turned{k}") for k in range(2)]
        sums_taken = [sem(f"sums_taken{k}") for k in range(2)]
        h_staged = sem("h_staged")
        h_turned = sem("h_turned")
        h_copied = sem("h_copied")
        projected = sem("projected")
        biased = sem("biased")
        l_staged = sem("l_staged")
        l_means = sem("l_means")
        l_count = sem("l_count")
        l_mean = sem("l_mean")
        l_turned = sem("l_turned")
        l_copied = sem("l_copied")
        l_hidden = sem("l_hidden")
        l_relu = sem("l_relu")
        l_out = sem("l_out")
        l_rows = sem("l_rows")
        stored = sem("stored")

        def over_groups(eng, body):
            with eng.Fori(0, NG // RING) as n:
                for r in range(RING):
                    body(n * RING + r, n, r)
            for r in range(NG % RING):
                body(NG // RING * RING + r, NG // RING, r)

        def over_chunks(eng, body):
            with eng.Fori(0, NCH // 2) as n:
                for b in range(2):
                    body(n * 2 + b, b)

        def group_plan(eng, g):
            first = eng.value_load(plan[0:1, bass.ds(g, 1), 0:1], min_val=0, max_val=n_nodes)
            count = eng.value_load(plan[0:1, bass.ds(g, 1), 1:2], min_val=1, max_val=n_nodes // WINDOW + 1)
            before = eng.value_load(plan[0:1, bass.ds(g, 1), 2:3], min_val=0,
                                    max_val=NG * (n_nodes // WINDOW + 1))
            return first, count, before

        def tiled(dram):
            return dram.rearrange("(t p) d -> p t d", p=P)

        def chunk_of(dram, c):
            return dram.rearrange("(c t p) d -> c p t d", p=P, t=CHUNK)[bass.ds(c, 1)]\
                .rearrange("c p t d -> (c p) t d")

        def rows_at(buffer, c):
            return buffer[:, bass.ds(c * CHUNK, CHUNK), :]

        def flat(buffer):
            return buffer[:].rearrange("p t d -> p (t d)")

        block = ctx.enter_context(nc.Block())

        @block.sync
        def _(sp):
            sp.dma_start(dst_i, dst).then_inc(dst_loaded, 16)
            sp.dma_start(x_rows[:], tiled(x)).then_inc(x_loaded, 16)
            sp.dma_start(flat(src_all)[:, 0:NG * TILES], src).then_inc(src_loaded, 16)
            sp.wait_ge(consts, 1)
            for here, there in (
                (w_attr[0:D, 0:D], w1a[D:2 * D, :]), (w_attr[D:2 * D, D:2 * D], w1a[D:2 * D, :]),
                (w_node[:], w1a[0:D, :]), (b1a_all[:], b1a.rearrange("(a d) -> a d", a=1).to_broadcast([P, D])),
                (w1b_b[0:D, :], w1b), (w1b_b[D:D + 1, :], b1b.rearrange("(a d) -> a d", a=1)),
                (w2a_h[:], w2a[0:D, :]), (w2a_m[:], w2a[D:2 * D, :]),
                (b2a_col[:], b2a.rearrange("(d a) -> d a", a=1)),
                (w2b_b[0:D, :], w2b), (w2b_b[D:D + 1, :], b2b.rearrange("(a d) -> a d", a=1)),
            ):
                sp.dma_start(here, there).then_inc(weights_loaded, 16)

            sp.wait_ge(norm_step[0], 6)
            sp.dma_start(tiled(tables[0]), rows[:]).then_inc(table_stored[0], 16)
            with sp.Fori(0, NCH) as c:
                sp.wait_ge(sums_taken[0], c + 3)
                sp.dma_start(chunk_of(tables[1], c), rows_at(rows, c)).then_inc(table_stored[1], 16)
            with sp.Fori(0, NCH) as c:
                sp.wait_ge(biased, c + 3)
                sp.dma_start(chunk_of(tables[2], c),
                             rows_at(table_rows.rearrange("p (t d) -> p t d", d=D), c))\
                    .then_inc(table_stored[2], 16)

            def load_attr(g, n, r):
                sp.wait_ge(multiplied, g + 1)
                sp.dma_start(attr_ring[:, r, :], attr[bass.ds(g, 1)].rearrange("g p e -> (g p) e"))\
                    .then_inc(attr_loaded[r], 16)
            over_groups(sp, load_attr)

            whole = FULL // CHUNK
            with sp.Fori(0, whole) as c:
                sp.wait_ge(l_rows, c + 2)
                sp.dma_start(chunk_of(out[0:whole * CHUNK * P, :], c), rows_at(rows, c)).then_inc(stored, 16)
            sp.wait_ge(l_rows, NCH + 1)
            if FULL > whole * CHUNK:
                sp.dma_start(tiled(out[whole * CHUNK * P:FULL * P, :]), rows[:, whole * CHUNK:FULL, :])\
                    .then_inc(stored, 16)
            if REST:
                sp.dma_start(out[FULL * P:n_nodes, :], rows[0:REST, FULL, :]).then_inc(stored, 16)
            sp.wait_ge(stored, 16 * (whole + (FULL > whole * CHUNK) + (REST > 0)))

        @block.gpsimd
        def _(pool):
            nc.gpsimd.memset(ident[:], 0.0).then_inc(pool_consts, 1)
            nc.gpsimd.memset(flat(src_all)[:, NG * TILES:], 0).then_inc(pool_consts, 1)
            nc.gpsimd.iota(node_no[:], pattern=[[1, COLS]], base=0, channel_multiplier=0)\
                .then_inc(pool_consts, 1)
            pool.wait_ge(pool_consts, 3)
            nc.gpsimd.affine_select(out=ident[:], in_=ident[:], compare_op=ALU.not_equal, fill=1.0, base=0,
                                    pattern=[[-1, P]], channel_multiplier=1).then_inc(pool_consts, 1)
            pool.wait_ge(plan_step, 4)
            nc.gpsimd.partition_all_reduce(span_all, span, P, RMAX).then_inc(spans_reduced, 1)

            for k in range(3):
                pool.wait_ge(table_stored[k], 16 if k == 0 else 16 * NCH)

                def gather(g, n, r):
                    pool.wait_ge(indices_staged[k], g + 1)
                    pool.nop(nofuse=True)
                    for j in range(TILES):
                        pool.indirect_dma_start(
                            ring[:, r, j, :], None, tables[k],
                            bass.IndirectOffsetOnAxis(ap=staged[:, r, j:j + 1], axis=0),
                        ).then_inc(gathered[k][r], 16)
                over_groups(pool, gather)

        @block.scalar
        def _(act):
            def deviation(k):
                act.wait_ge(norm_step[k], 5)
                nc.scalar.activation(col_b[:], col_a[:], ACT.Sqrt, bias=eps[:], scale=1.0 / D)\
                    .then_inc(std_ready[k], 1)

            def sweep(k):
                if k:
                    act.wait_ge(gathered[k - 1][(NG - 1) % RING], GROUP_LANDED * (NG // RING + 1))
                nc.scalar.copy(staged[:].rearrange("p r t -> p (r t)"), flat(src_all)[:, 0:RING * TILES])\
                    .then_inc(indices_staged[k], RING)

                def body(g, n, r):
                    act.wait_ge(slot_free[k], g + 3)
                    act.nop(nofuse=True)
                    nc.scalar.copy(staged[:, r, :],
                                   flat(src_all)[:, bass.ds((g + RING) * TILES, TILES)])\
                        .then_inc(indices_staged[k], 1)
                    if k == 2:
                        act.wait_ge(msg_used, g + 1)
                        nc.scalar.activation(
                            msg[:, r % 2, :, 0:D], pre[:, r % 2, :].rearrange("p (t d) -> p t d", d=D),
                            ACT.Relu).then_inc(msg_ready, 1)
                over_groups(act, body)

            def stage_sums(k):
                act.wait_ge(slot_free[k], NG + 2)

                def body(c, b):
                    act.wait_ge(sums_turned[k], c + 1)
                    act.nop(nofuse=True)
                    nc.scalar.activation(stage_t[:, b, :], sums[0:D, bass.ds(c * CW, CW)],
                                         ACT.Relu if k == 0 else ACT.Copy).then_inc(sums_staged[k], 1)
                over_chunks(act, body)

            act.wait_ge(consts, 3)
            deviation(0)
            act.wait_ge(src_loaded, 16)
            act.wait_ge(pool_consts, 4)
            sweep(0)
            stage_sums(0)
            sweep(1)
            stage_sums(1)
            deviation(1)
            act.wait_ge(norm_step[1], 6)

            def stage_h(c, b):
                act.wait_ge(h_turned, c + 1)
                act.nop(nofuse=True)
                nc.scalar.copy(stage_r[:, b, :], flat(rows)[:, bass.ds(c * RW, RW)]).then_inc(h_staged, 1)
                act.wait_ge(h_turned, c + 3)
                act.wait_ge(projected, c + 1)
                nc.scalar.copy(h_t[:], psum[0:D, 0:CW]).then_inc(h_copied, 1)
            over_chunks(act, stage_h)
            act.sem_inc(msg_ready, 2)
            sweep(2)

            act.wait_ge(msg_used, NG + 2)

            def layer(c, b):
                act.wait_ge(l_turned, c + 1)
                act.nop(nofuse=True)
                nc.scalar.copy(stage_r[:, b, :], flat(rows)[:, bass.ds(c * RW, RW)]).then_inc(l_staged, 1)
                act.wait_ge(l_turned, c + 3)
                act.wait_ge(l_hidden, c + 1)
                nc.scalar.copy(h_t[:], bank(4, CW)[0:D, :]).then_inc(l_copied, 1)
                act.wait_ge(l_hidden, c + 2)
                act.wait_ge(l_out, c + 1)
                nc.scalar.activation(hid_t[0:D, :], bank(6, CW)[0:D, :], ACT.Relu, bias=b2a_col[:])\
                    .then_inc(l_relu, 1)
            over_chunks(act, layer)

        @block.tensor
        def _(pe):
            def scatter(k, g, values, width):
                first, count, before = group_plan(pe, g)
                with pe.Fori(0, count) as v:
                    pe.wait_ge(hit_built[k], before + v + 1)
                    pe.wait_ge(summed[k], before + v + 1)
                    pe.nop(nofuse=True)
                    for j in range(TILES):
                        mm = pe.matmul(bank(2, WINDOW)[0:width, :], values[:, j, 0:width], hit[:, j, :],
                                       start=(j == 0), stop=(j == TILES - 1))
                    mm.then_inc(scattered[k], 1)

            def by_banks(matmul):
                for a in range(0, CW, BANK):
                    mm = matmul(a, min(CW, a + BANK))
                return mm

            pe.wait_ge(weights_loaded, 16 * 11)
            pe.wait_ge(pool_consts, 4)
            pe.wait_ge(consts, 3)
            pe.wait_ge(plan_ready, 1)
            for k in range(2):
                def sum_rows(g, n, r):
                    pe.wait_ge(gathered[k][r], GROUP_LANDED * (n + 1))
                    scatter(k, g, ring[:, r], D)
                over_groups(pe, sum_rows)
                pe.sem_inc(sums_turned[k], 2)

                def turn(c, b):
                    pe.wait_ge(sums_staged[k], c + 1)
                    pe.wait_ge(sums_taken[k], c + 1)
                    pe.nop(nofuse=True)
                    for t in range(CHUNK):
                        mm = pe.transpose(bank(b)[:, t * D:(t + 1) * D], stage_t[:, b, t * P:(t + 1) * P],
                                          ident[0:D, 0:D])
                    mm.then_inc(sums_turned[k], 1)
                over_chunks(pe, turn)

            pe.sem_inc(h_turned, 2)
            pe.sem_inc(projected, 1)
            pe.sem_inc(h_copied, 1)

            def project(c, b):
                pe.wait_ge(h_staged, c + 1)
                pe.wait_ge(h_copied, c + 1)
                pe.nop(nofuse=True)
                for t in range(CHUNK):
                    mm = pe.transpose(psum[0:D, t * P:(t + 1) * P], stage_r[:, b, t * D:(t + 1) * D], ident[:])
                mm.then_inc(h_turned, 1)
                pe.wait_ge(h_copied, c + 2)
                pe.wait_ge(biased, c + 1)
                pe.nop(nofuse=True)
                for t in range(CHUNK):
                    mm = pe.matmul(bank(2 + b)[:, t * D:(t + 1) * D], h_t[:, t * P:(t + 1) * P], w_node[:],
                                   start=True, stop=True)
                mm.then_inc(projected, 1)
            over_chunks(pe, project)

            pe.sem_inc(multiplied, RING)

            def messages(g, n, r):
                pe.wait_ge(attr_loaded[r], 16 * (n + 1))
                pe.wait_ge(slot_free[2], g + 1)
                for j in range(TILES // 2):
                    mm = pe.matmul(bank(r % 2)[:, j * P:(j + 1) * P],
                                   attr_ring[:, r, j * TILE:(j + 1) * TILE], w_attr[:], start=True, stop=True)
                mm.then_inc(multiplied, 1)
                pe.wait_ge(msg_ready, g + 3)
                scatter(2, g, msg[:, r % 2], D + 1)
            over_groups(pe, messages)

            pe.wait_ge(msg_used, NG + 2)
            pe.sem_inc(l_turned, 2)
            pe.sem_inc(l_hidden, 1)
            pe.sem_inc(l_out, 1)

            def layer(c, b):
                pe.wait_ge(l_rows, c + 1)
                pe.nop(nofuse=True)
                by_banks(lambda a, z: pe.matmul(psum[0:D, a:z], w1b_b[:], sums[:, bass.ds(c * CW + a, z - a)],
                                                start=True, stop=True))
                by_banks(lambda a, z: pe.matmul(psum[0:D, 2 * BANK + a:2 * BANK + z], count_all[:],
                                                sums[:, bass.ds(c * CW + a, z - a)],
                                                start=True, stop=True)).then_inc(l_means, 1)
                pe.wait_ge(l_staged, c + 1)
                pe.wait_ge(l_copied, c + 1)
                pe.nop(nofuse=True)
                for t in range(CHUNK):
                    mm = pe.transpose(bank(4, CW)[0:D, t * P:(t + 1) * P], stage_r[:, b, t * D:(t + 1) * D],
                                      ident[:])
                mm.then_inc(l_turned, 1)
                pe.wait_ge(l_copied, c + 2)
                pe.wait_ge(l_relu, c + 1)
                pe.nop(nofuse=True)
                by_banks(lambda a, z: pe.matmul(psum[0:D, 6 * BANK + a:6 * BANK + z], w2a_h[:], h_t[:, a:z],
                                                start=True, stop=False))
                pe.wait_ge(l_mean, c + 2)
                pe.nop(nofuse=True)
                by_banks(lambda a, z: pe.matmul(psum[0:D, 6 * BANK + a:6 * BANK + z], w2a_m[:], mean_t[:, a:z],
                                                start=False, stop=True)).then_inc(l_hidden, 1)
                pe.wait_ge(l_relu, c + 2)
                pe.nop(nofuse=True)
                for t in range(CHUNK):
                    mm = pe.matmul(bank(0)[:, t * D:(t + 1) * D], hid_t[:, t * P:(t + 1) * P], w2b_b[:],
                                   start=True, stop=True)
                mm.then_inc(l_out, 1)
            over_chunks(pe, layer)

        @block.vector
        def _(dve):
            def norm(k):
                rows3 = work.rearrange("p (t d) -> p t d", d=D)

                def spread(col):
                    return col[:].unsqueeze(2).to_broadcast([P, NT, D])

                nc.vector.tensor_reduce(col_a[:], x_rows[:], AX.X, ALU.add).then_inc(norm_step[k], 1)
                dve.wait_ge(norm_step[k], 1)
                nc.vector.tensor_scalar(col_b[:], col_a[:], 1.0 / D, None, ALU.mult).then_inc(norm_step[k], 1)
                dve.wait_ge(norm_step[k], 2)
                nc.vector.tensor_tensor(rows3, x_rows[:], spread(col_b), ALU.subtract)\
                    .then_inc(norm_step[k], 1)
                dve.wait_ge(norm_step[k], 3)
                nc.vector.tensor_tensor(flat(rows), work, work, ALU.mult).then_inc(norm_step[k], 1)
                dve.wait_ge(norm_step[k], 4)
                nc.vector.tensor_reduce(col_a[:], rows[:], AX.X, ALU.add).then_inc(norm_step[k], 1)
                dve.wait_ge(std_ready[k], 1)
                nc.vector.reciprocal(col_a[:], col_b[:]).then_inc(std_ready[k], 1)
                dve.wait_ge(std_ready[k], 2)
                nc.vector.scalar_tensor_tensor(out=rows[:], in0=rows3, scalar=0.0, in1=spread(col_a),
                                               op0=ALU.max, op1=ALU.mult).then_inc(norm_step[k], 1)

            nc.vector.memset(w_attr[:], 0.0).then_inc(consts, 1)
            nc.vector.memset(eps[:], EPS)
            nc.vector.memset(count_all[0:D, :], 0.0)
            nc.vector.memset(count_all[D:D + 1, :], 1.0)
            nc.vector.memset(hid_t[D:D + 1, :], 1.0)
            nc.vector.memset(tick[:], 0.0)
            nc.vector.memset(msg[:, :, :, D:D + 1], 1.0).then_inc(consts, 1)

            dst_f = flat(dst_rel)
            dve.wait_ge(dst_loaded, 16)
            nc.vector.tensor_copy(dst_f, dst_i).then_inc(plan_step, 1)
            dve.wait_ge(plan_step, 1)
            nc.vector.tensor_reduce(span[:, 0:NG], dst_rel[:], AX.X, ALU.max).then_inc(plan_step, 1)
            nc.vector.tensor_reduce(windows, dst_rel[:], AX.X, ALU.min).then_inc(plan_step, 1)
            dve.wait_ge(plan_step, 3)
            nc.vector.tensor_scalar(span[:, NG:2 * NG], windows, -1.0, None, ALU.mult).then_inc(plan_step, 1)
            dve.wait_ge(plan_step, 4)
            nc.vector.tensor_scalar(eps[:], eps[:], 1.0, None, ALU.mult).then_inc(consts, 1)
            dve.wait_ge(x_loaded, 16)
            norm(0)
            dve.wait_ge(spans_reduced, 1)
            nc.vector.tensor_tensor(dst_rel[:], dst_rel[:], minus_first.unsqueeze(2).to_broadcast([P, NG, TILES]),
                                    ALU.add).then_inc(plan_step, 1)
            nc.vector.tensor_tensor(windows_i, last, minus_first, ALU.add).then_inc(plan_step, 1)
            dve.wait_ge(plan_step, 6)
            nc.vector.tensor_scalar(windows_i, windows_i, SHIFT, None, ALU.logical_shift_right)\
                .then_inc(plan_step, 1)
            dve.wait_ge(plan_step, 7)
            nc.vector.tensor_scalar(windows, windows_i, 1.0, None, ALU.add).then_inc(plan_step, 1)
            dve.wait_ge(plan_step, 8)
            nc.vector.memset(span[:, 0:NG], 1.0).then_inc(plan_step, 1)
            dve.wait_ge(plan_step, 9)
            nc.vector.tensor_tensor_scan(visits, span[:, 0:NG], windows, 0.0, ALU.mult, ALU.add)\
                .then_inc(plan_step, 1)
            dve.wait_ge(plan_step, 10)
            nc.vector.tensor_tensor(plan[0:1, :, 2], visits[0:1, :], windows[0:1, :], ALU.subtract)
            nc.vector.tensor_copy(plan[0:1, :, 1], windows[0:1, :])
            nc.vector.tensor_scalar(plan[0:1, :, 0], minus_first[0:1, :], -1.0, None, ALU.mult)\
                .then_inc(plan_step, 1)
            dve.wait_ge(plan_step, 11)
            dve.wait_ge(pool_consts, 4)
            nc.vector.tensor_copy(tick[:], tick[:]).then_inc(plan_ready, 1)

            def sweep(k):
                width = D if k < 2 else D + 1
                nc.vector.memset(arena[:], 0.0).then_inc(summed[k], 1)
                dve.sem_inc(slot_free[k], 2)
                if k == 2:
                    dve.sem_inc(msg_used, 2)

                def body(g, n, r):
                    first, count, before = group_plan(dve, g)
                    if k == 2:
                        dve.wait_ge(multiplied, g + 1 + RING)
                        dve.wait_ge(gathered[2][r], GROUP_LANDED * (n + 1))
                        dve.wait_ge(msg_ready, g + 1)
                        nc.vector.tensor_tensor(pre[:, r % 2, :], bank(r % 2),
                                                ring[:, r].rearrange("p t d -> p (t d)"), ALU.add)\
                            .then_inc(slot_free[2], 1)
                    with dve.Fori(0, count) as v:
                        nc.vector.tensor_tensor(
                            hit[:],
                            node_no[:, bass.ds(v * WINDOW, WINDOW)].unsqueeze(1)
                            .to_broadcast([P, TILES, WINDOW]),
                            dst_rel[:, bass.ds(g, 1), :].rearrange("p g t -> p (g t)").unsqueeze(2)
                            .to_broadcast([P, TILES, WINDOW]),
                            ALU.is_equal).then_inc(hit_built[k], 1)
                        begin = nc.s_assert_within(first + v * WINDOW, 0, COLS - WINDOW,
                                                   skip_runtime_bounds_check_because="the span is within the nodes")
                        window = sums[0:width, bass.ds(begin, WINDOW)]
                        dve.wait_ge(scattered[k], before + v + 1)
                        dve.wait_ge(summed[k], before + v + 1)
                        dve.nop(nofuse=True)
                        nc.vector.tensor_tensor(window, window, bank(2, WINDOW)[0:width, :], ALU.add)\
                            .then_inc(summed[k], 1)
                    nc.vector.tensor_copy(tick[:], tick[:]).then_inc(slot_free[k] if k < 2 else msg_used, 1)
                over_groups(dve, body)

            for k in range(2):
                if k:
                    dve.wait_ge(sums_staged[0], NCH)
                sweep(k)
                dve.sem_inc(sums_taken[k], 2)

                def take(c, b):
                    dve.wait_ge(sums_turned[k], c + 3)
                    dve.nop(nofuse=True)
                    turned = bank(b, RW).rearrange("p (t d) -> p t d", d=D)
                    if k == 0:
                        nc.vector.tensor_copy(rows_at(rows, c), turned).then_inc(sums_taken[0], 1)
                    else:
                        nc.vector.tensor_tensor(rows_at(x_rows, c), rows_at(x_rows, c), turned, ALU.add)\
                            .then_inc(sums_taken[1], 1)
                over_chunks(dve, take)
            dve.wait_ge(sums_taken[1], NCH + 2)
            dve.wait_ge(table_stored[1], 16 * NCH)
            norm(1)
            dve.sem_inc(biased, 2)

            def bias(c, b):
                dve.wait_ge(projected, c + 2)
                dve.nop(nofuse=True)
                nc.vector.tensor_tensor(rows_at(table_rows.rearrange("p (t d) -> p t d", d=D), c),
                                        bank(2 + b, RW).rearrange("p (t d) -> p t d", d=D),
                                        b1a_all[:].unsqueeze(1).to_broadcast([P, CHUNK, D]), ALU.add)\
                    .then_inc(biased, 1)
            over_chunks(dve, bias)
            dve.wait_ge(table_stored[2], 16 * NCH)
            sweep(2)

            dve.sem_inc(l_mean, 1)
            dve.sem_inc(l_rows, 1)
            dve.sem_inc(l_relu, 1)
            dve.sem_inc(l_copied, 1)

            def layer(c, b):
                dve.wait_ge(l_means, c + 1)
                dve.wait_ge(l_hidden, c + 1)
                nc.vector.tensor_scalar(inv_count, psum[0:D, 2 * BANK:2 * BANK + CW], 1.0, None, ALU.max)\
                    .then_inc(l_count, 1)
                dve.wait_ge(l_count, c * 2 + 1)
                nc.vector.reciprocal(inv_count, inv_count).then_inc(l_count, 1)
                dve.wait_ge(l_count, c * 2 + 2)
                nc.vector.tensor_tensor(mean_t, psum[0:D, 0:CW], inv_count, ALU.mult).then_inc(l_mean, 1)
                dve.wait_ge(l_out, c + 2)
                dve.nop(nofuse=True)
                nc.vector.tensor_tensor(rows_at(rows, c), bank(0, RW).rearrange("p (t d) -> p t d", d=D),
                                        rows_at(x_rows, c), ALU.add).then_inc(l_rows, 1)
            over_chunks(dve, layer)


def kernel(x, src, dst, edge_attr_64, L1_gnn_u, L1_gnn_w1a, L1_gnn_b1a, L1_gnn_w1b, L1_gnn_b1b,
           L1_gnn_w2a, L1_gnn_b2a, L1_gnn_w2b, L1_gnn_b2b):
    import numpy as _np
    import concourse.bacc as _bacc
    from concourse import mybir as _mybir
    from concourse.bass_utils import run_bass_kernel_spmd as _run

    n_nodes, d = x.shape
    n_edges = src.shape[0]
    node_rows = -(-n_nodes // (P * CHUNK)) * P * CHUNK
    groups = -(-n_edges // (TILE * TILES))
    n_pad = groups * TILE * TILES - n_edges

    def by_partition(index, fill):
        a = _np.concatenate([_np.asarray(index), _np.full(n_pad, fill, _np.asarray(index).dtype)])
        return _np.ascontiguousarray(a.reshape(groups, TILE, TILES).transpose(1, 0, 2).reshape(TILE, -1))

    attr = _np.concatenate([_np.asarray(edge_attr_64), _np.zeros((n_pad, d), _np.float32)])
    attr = attr.reshape(groups, TILE, TILES // 2, 2, d).transpose(0, 3, 4, 2, 1)
    arrays = {
        "x": _np.concatenate([_np.asarray(x), _np.zeros((node_rows - n_nodes, d), _np.float32)]),
        "src": by_partition(src, 0),
        "dst": by_partition(dst, n_nodes),
        "attr": _np.ascontiguousarray(attr.reshape(groups, 2 * d, TILES // 2 * TILE)),
        "w1a": L1_gnn_w1a, "b1a": L1_gnn_b1a, "w1b": L1_gnn_w1b, "b1b": L1_gnn_b1b,
        "w2a": L1_gnn_w2a, "b2a": L1_gnn_b2a, "w2b": L1_gnn_w2b, "b2b": L1_gnn_b2b,
    }
    arrays = {n: _np.ascontiguousarray(a) for n, a in arrays.items()}
    nc = _bacc.Bacc("TRN2", target_bir_lowering=False, num_devices=1)
    args = [nc.dram_tensor(f"in_{n}", a.shape, _mybir.dt.from_np(a.dtype), kind="ExternalInput").ap()
            for n, a in arrays.items()]
    out = nc.dram_tensor("out_0", (n_nodes, d), _mybir.dt.float32, kind="ExternalOutput").ap()
    gnn_kernel(nc, *args, out)
    r = _run(nc, [{f"in_{n}": a for n, a in arrays.items()}], core_ids=[0])
    return r.results[0]["out_0"]
```

```python
from contextlib import ExitStack

import concourse.bass as bass
from concourse import mybir

P = 128
TILE = 128
TILES = 8
RING = 4
WINDOW = 64
SPAN = 7
TPS = 18
WIDE = 96
GATHERED = 196
LAG = 3
BY_VECTOR = (3, 8, 13)
CHUNK = 7
EPS = 1e-5

ALU = mybir.AluOpType
ACT = mybir.ActivationFunctionType
F32 = mybir.dt.float32
I32 = mybir.dt.int32
I16 = mybir.dt.int16
BF16 = mybir.dt.bfloat16
U32 = mybir.dt.uint32
AX = mybir.AxisListType
RMAX = bass.bass_isa.ReduceOp.max


def gnn_kernel(nc, x, src, dst, src_c, dst_c, attr, w1a, b1a, w1b, b1b, w2a, b2a, w2b, b2b, out):
    n_nodes, D = out.shape
    NT = x.shape[0] // P
    NCH = NT // CHUNK
    NG = attr.shape[0]
    CW = CHUNK * P
    RW = CHUNK * D
    BANK = 512
    COLS = NT * P + WINDOW
    GROUP_LANDED = 16 * TILES
    SHIFT = WINDOW.bit_length() - 1
    FULL = n_nodes // P
    REST = n_nodes - FULL * P
    assert NCH * CHUNK == NT and NCH % 2 == 0 and TILES * D <= BANK and RW <= BANK and CW <= 2 * BANK
    NC = src_c.shape[1]
    NS = NC // TPS
    KEYS = SPAN * NT
    HK = KEYS // 2
    ACT_TILES = [t for t in range(TPS) if t not in BY_VECTOR]
    assert NS * TPS == NC and NS % 2 == 0 and NS > 4 and GATHERED >= 2 * NS and GATHERED % RING == 0
    assert GATHERED * TILES + NC == NG * TILES and HK * 2 == KEYS and HK <= BANK and TPS * SPAN <= P
    assert RING == 4 and TPS % 2 == 0 and NS <= P
    assert n_nodes < NT * P and WINDOW == 1 << SHIFT and NG % RING and TILE == P

    with ExitStack() as ctx:
        def sb(name, shape, dt=F32):
            return ctx.enter_context(nc.sbuf_tensor(name, shape, dt))

        def sem(name):
            return ctx.enter_context(nc.semaphore(name))

        tables = [nc.dram_tensor(f"table{k}", [NT * P, D], F32).ap() for k in range(3)]
        psum = ctx.enter_context(nc.psum_tensor("psum", [P, 8 * BANK], F32))

        def bank(b, width=BANK):
            return psum[:, b * BANK:b * BANK + width]

        src_all = sb("src_all", [P, NG + RING, TILES], I16)
        dst_rel = sb("dst_rel", [P, NG, TILES], I16)
        plan = sb("plan", [P, NG, 3], I32)
        number = sb("number", [P, KEYS], I16)
        staged = sb("staged", [P, RING, TILES], U32)
        ring = sb("ring", [P, RING, TILES, D])
        rel_now = sb("rel_now", [P, TILES])
        hit = sb("hit", [P, TILES, WINDOW])
        tick = sb("tick", [P, 5])
        tick_i = sb("tick_i", [P, 1], I32)

        keys = sb("keys", [P, NS + 1, 2, TPS])
        keys_now = sb("keys_now", [P, 2, 2, TPS])
        low_ring = sb("low_ring", [P, RING, P], BF16)
        key_ring = sb("key_ring", [P, RING, KEYS], BF16)
        slot_node = sb("slot_node", [P, NS])
        plan_c = sb("plan_c", [P, NS], I32)
        wide = sb("wide", [P, 1], I32)
        parts = sb("parts", [P, D])
        hit_c = sb("hit_c", [P, WIDE])
        mask = sb("mask", [P, TPS])
        part_no = sb("part_no", [P, 1])
        ones = sb("ones", [P, P])
        limits = sb("limits", [P, 2, 4])
        col_min = sb("col_min", [P, TPS])
        col_max = sb("col_max", [P, TPS])

        x_rows = sb("x_rows", [P, NT, D])
        rows = sb("rows", [P, NT, D])
        arena = sb("arena", [P, COLS])
        thirds = sb("thirds", [P, NT, 3, D], BF16)
        col_a = sb("col_a", [P, NT])
        col_b = sb("col_b", [P, NT])
        stage_t = sb("stage_t", [D, 2, CW])
        inv_count = stage_t[:, 0, :]
        mean_t = stage_t[:, 1, :]
        counts = [flat_[:].rearrange("p t d -> p (t d)").bitcast(BF16) for flat_ in (rows, x_rows)]

        thirds_f = thirds[:].rearrange("p t a d -> p (t a d)").bitcast(F32)
        used = [0]

        def in_thirds(n, partitions=P):
            used[0] += n
            assert used[0] <= NT * 3 * D // 2
            return thirds_f[0:partitions, used[0] - n:used[0]]

        src_i = in_thirds(NG * TILES).bitcast(I32)
        dst_t = in_thirds(NC)
        src_t = in_thirds(NC).bitcast(I32)
        first_t = in_thirds(NC)
        used[0] = 0
        attr_ring = in_thirds(RING * TILES // 2 * TILE).rearrange("p (r e) -> p r e", r=RING)
        pre = in_thirds(2 * TILES * D).rearrange("p (b e) -> p b e", b=2)
        msg = in_thirds(2 * TILES * (D + 1)).rearrange("p (b t d) -> p b t d", b=2, t=TILES)
        stage_r = in_thirds(2 * RW).rearrange("p (b e) -> p b e", b=2)
        h_t = in_thirds(CW, D)
        hid_t = in_thirds(CW, D + 1)

        sums = arena[0:D + 1, :]
        work = arena[:, 0:NT * D]
        LIMITS = 24 + -(-TPS // 4)
        table_rows = arena[:, NT * D:2 * NT * D]
        at_ = [NT * D]

        def scratch(n):
            at_[0] += n
            return arena[:, at_[0] - n:at_[0]]

        dst_i = scratch(NG * TILES).bitcast(I32)
        span = scratch(2 * NG)
        span_all = scratch(2 * NG)
        windows_i = scratch(NG).bitcast(I32)
        windows = scratch(NG)
        visits = scratch(NG)
        assert at_[0] <= COLS
        last, minus_first = span_all[:, 0:NG], span_all[:, NG:2 * NG]

        ident = sb("ident", [P, P])
        eps = sb("eps", [P, 1])
        w_attr = sb("w_attr", [P, 2 * D])
        w_node = sb("w_node", [D, D])
        b1a_all = sb("b1a_all", [P, D])
        w1b_b = sb("w1b_b", [D + 1, D])
        count_all = sb("count_all", [D + 1, D])
        w2a_h = sb("w2a_h", [D, D])
        w2a_m = sb("w2a_m", [D, D])
        b2a_col = sb("b2a_col", [D, 1])
        w2b_b = sb("w2b_b", [D + 1, D])

        dst_loaded = sem("dst_loaded")
        x_loaded = sem("x_loaded")
        src_loaded = sem("src_loaded")
        src_narrowed = sem("src_narrowed")
        weights_loaded = sem("weights_loaded")
        pool_consts = sem("pool_consts")
        consts = sem("consts")
        plan_step = sem("plan_step")
        spans_reduced = sem("spans_reduced")
        plan_ready = sem("plan_ready")
        norm_step = [sem(f"norm_step{k}") for k in range(2)]
        std_ready = [sem(f"std_ready{k}") for k in range(2)]
        table_stored = [sem(f"table_stored{k}") for k in range(3)]
        plan_c_step = sem("plan_c_step")
        tiles_turned = sem("tiles_turned")
        firsts_spread = sem("firsts_spread")
        limits_reduced = sem("limits_reduced")
        src_c_loaded = sem("src_c_loaded")
        dst_c_loaded = sem("dst_c_loaded")
        x_again = sem("x_again")
        late_consts = sem("late_consts")
        split_step = [sem(f"split_step{k}") for k in range(2)]
        sweep_done = [sem(f"sweep_done{k}") for k in range(3)]
        rel_step = [sem(f"rel_step{k}") for k in range(3)]
        keys_staged = [sem(f"keys_staged{k}") for k in range(2)]
        marked = [sem(f"marked{k}") for k in range(2)]
        counted = [sem(f"counted{k}") for k in range(2)]
        copied_a = [sem(f"copied_a{k}") for k in range(2)]
        copied_v = [sem(f"copied_v{k}") for k in range(2)]
        applied = [sem(f"applied{k}") for k in range(2)]
        parts_ready = [sem(f"parts_ready{k}") for k in range(2)]
        placed = [sem(f"placed{k}") for k in range(2)]
        indices_staged = [sem(f"indices_staged{k}") for k in range(3)]
        gathered = [[sem(f"gathered{k}_{r}") for r in range(RING)] for k in range(3)]
        slot_free = [sem(f"slot_free{k}") for k in range(3)]
        hit_built = [sem(f"hit_built{k}") for k in range(3)]
        scattered = [sem(f"scattered{k}") for k in range(3)]
        summed = [sem(f"summed{k}") for k in range(3)]
        attr_loaded = [sem(f"attr_loaded{r}") for r in range(RING)]
        multiplied = sem("multiplied")
        msg_ready = sem("msg_ready")
        msg_used = sem("msg_used")
        sums_staged = [sem(f"sums_staged{k}") for k in range(2)]
        sums_turned = [sem(f"sums_turned{k}") for k in range(2)]
        sums_taken = [sem(f"sums_taken{k}") for k in range(2)]
        h_staged = sem("h_staged")
        h_turned = sem("h_turned")
        h_copied = sem("h_copied")
        projected = sem("projected")
        biased = sem("biased")
        l_staged = sem("l_staged")
        l_means = sem("l_means")
        l_count = sem("l_count")
        l_mean = sem("l_mean")
        l_turned = sem("l_turned")
        l_copied = sem("l_copied")
        l_hidden = sem("l_hidden")
        l_relu = sem("l_relu")
        l_out = sem("l_out")
        l_rows = sem("l_rows")
        stored = sem("stored")

        def over_groups(eng, body):
            with eng.Fori(0, NG // RING) as n:
                for r in range(RING):
                    body(n * RING + r, n, r)
            for r in range(NG % RING):
                body(NG // RING * RING + r, NG // RING, r)

        def over_chunks(eng, body):
            with eng.Fori(0, NCH // 2) as n:
                for b in range(2):
                    body(n * 2 + b, b)

        def group_plan(eng, g):
            first = eng.value_load(plan[0:1, bass.ds(g, 1), 0:1], min_val=0, max_val=n_nodes)
            count = eng.value_load(plan[0:1, bass.ds(g, 1), 1:2], min_val=1, max_val=n_nodes // WINDOW + 1)
            before = eng.value_load(plan[0:1, bass.ds(g, 1), 2:3], min_val=0,
                                    max_val=NG * (n_nodes // WINDOW + 1))
            return first, count, before

        def tile_copied(eng, k, s, t):
            if t < 0:
                s, t = s - 1, t + TPS
            if t in BY_VECTOR:
                eng.wait_ge(copied_v[k], s * len(BY_VECTOR) + BY_VECTOR.index(t) + 2)
            else:
                eng.wait_ge(copied_a[k], s * len(ACT_TILES) + ACT_TILES.index(t) + 2)

        def sums_before(s):
            return s * 3 - 2 if not isinstance(s, int) or s > 1 else s + 1

        def tile_counts(t):
            return psum[:, t % 2 * 2 * BANK:(t % 2 * 2 + 2) * BANK].rearrange("p (a e) -> p a e", a=2)[:, :, 0:HK]

        def slot_counts(b, t):
            return counts[b][:, t * KEYS:(t + 1) * KEYS].rearrange("p (a e) -> p a e", a=2)

        def over_supertiles(eng, body):
            for b in range(2):
                body(b, b, 0)
            with eng.Fori(1, NS // 2) as n:
                for b in range(2):
                    body(n * 2 + b, b, n)

        def over_late_groups(eng, body):
            with eng.Fori(NS // 2, GATHERED // RING) as n:
                for r in range(RING):
                    body(n * RING + r, n, r)
            assert NS // 2 < GATHERED // RING

        def either(eng, narrow, gather_all):
            flag = eng.value_load(wide[0:1, 0:1], min_val=0, max_val=1)
            with eng.If(flag == 0):
                narrow()
            with eng.Else():
                gather_all()

        def tiled(dram):
            return dram.rearrange("(t p) d -> p t d", p=P)

        def chunk_of(dram, c):
            return dram.rearrange("(c t p) d -> c p t d", p=P, t=CHUNK)[bass.ds(c, 1)]\
                .rearrange("c p t d -> (c p) t d")

        def rows_at(buffer, c):
            return buffer[:, bass.ds(c * CHUNK, CHUNK), :]

        def flat(buffer):
            return buffer[:].rearrange("p t d -> p (t d)")

        block = ctx.enter_context(nc.Block())

        @block.sync
        def _(sp):
            sp.dma_start(dst_i, dst).then_inc(dst_loaded, 16)
            sp.dma_start(x_rows[:], tiled(x)).then_inc(x_loaded, 16)
            sp.dma_start(dst_t.bitcast(I32), dst_c).then_inc(dst_c_loaded, 16)
            sp.dma_start(src_t, src_c).then_inc(src_c_loaded, 16)
            sp.dma_start(src_i, src).then_inc(src_loaded, 16)
            sp.wait_ge(consts, 1)
            for here, there in (
                (w_attr[0:D, 0:D], w1a[D:2 * D, :]), (w_attr[D:2 * D, D:2 * D], w1a[D:2 * D, :]),
                (w_node[:], w1a[0:D, :]), (b1a_all[:], b1a.rearrange("(a d) -> a d", a=1).to_broadcast([P, D])),
                (w1b_b[0:D, :], w1b), (w1b_b[D:D + 1, :], b1b.rearrange("(a d) -> a d", a=1)),
                (w2a_h[:], w2a[0:D, :]), (w2a_m[:], w2a[D:2 * D, :]),
                (b2a_col[:], b2a.rearrange("(d a) -> d a", a=1)),
                (w2b_b[0:D, :], w2b), (w2b_b[D:D + 1, :], b2b.rearrange("(a d) -> a d", a=1)),
            ):
                sp.dma_start(here, there).then_inc(weights_loaded, 16)

            sp.wait_ge(norm_step[0], 6)
            sp.dma_start(tiled(tables[0]), rows[:]).then_inc(table_stored[0], 16)
            with sp.Fori(0, NCH) as c:
                sp.wait_ge(sums_taken[0], c + 3)
                sp.dma_start(chunk_of(tables[1], c), rows_at(rows, c)).then_inc(table_stored[1], 16)
            sp.wait_ge(sweep_done[1], 1)
            sp.dma_start(x_rows[:], tiled(x)).then_inc(x_again, 16)
            with sp.Fori(0, NCH) as c:
                sp.wait_ge(biased, c + 3)
                sp.dma_start(chunk_of(tables[2], c),
                             rows_at(table_rows.rearrange("p (t d) -> p t d", d=D), c))\
                    .then_inc(table_stored[2], 16)

            def load_attr(g, n, r):
                sp.wait_ge(multiplied, g + 1)
                sp.dma_start(attr_ring[:, r, :], attr[bass.ds(g, 1)].rearrange("g p e -> (g p) e"))\
                    .then_inc(attr_loaded[r], 16)
            over_groups(sp, load_attr)

            whole = FULL // CHUNK
            with sp.Fori(0, whole) as c:
                sp.wait_ge(l_rows, c + 2)
                sp.dma_start(chunk_of(out[0:whole * CHUNK * P, :], c), rows_at(rows, c)).then_inc(stored, 16)
            sp.wait_ge(l_rows, NCH + 1)
            if FULL > whole * CHUNK:
                sp.dma_start(tiled(out[whole * CHUNK * P:FULL * P, :]), rows[:, whole * CHUNK:FULL, :])\
                    .then_inc(stored, 16)
            if REST:
                sp.dma_start(out[FULL * P:n_nodes, :], rows[0:REST, FULL, :]).then_inc(stored, 16)
            sp.wait_ge(stored, 16 * (whole + (FULL > whole * CHUNK) + (REST > 0)))

        @block.gpsimd
        def _(pool):
            nc.gpsimd.memset(ident[:], 0.0).then_inc(pool_consts, 1)
            nc.gpsimd.memset(flat(src_all)[:, NG * TILES:], 0).then_inc(pool_consts, 1)
            nc.gpsimd.memset(keys[:, NS], 0.0).then_inc(pool_consts, 1)
            nc.gpsimd.memset(mask[:], 1.0).then_inc(pool_consts, 1)
            nc.gpsimd.iota(number[:], pattern=[[1, KEYS]], base=0, channel_multiplier=0).then_inc(pool_consts, 1)
            nc.gpsimd.iota(tick_i[:], pattern=[[0, 1]], base=0, channel_multiplier=1).then_inc(pool_consts, 1)
            pool.wait_ge(pool_consts, 6)
            nc.gpsimd.affine_select(out=mask[:], in_=mask[:], compare_op=ALU.is_ge, fill=0.0, base=0,
                                    pattern=[[-SPAN, TPS]], channel_multiplier=1).then_inc(pool_consts, 1)
            pool.wait_ge(pool_consts, 7)
            nc.gpsimd.affine_select(out=mask[:], in_=mask[:], compare_op=ALU.is_ge, fill=0.0, base=SPAN - 1,
                                    pattern=[[SPAN, TPS]], channel_multiplier=-1).then_inc(pool_consts, 1)
            nc.gpsimd.affine_select(out=ident[:], in_=ident[:], compare_op=ALU.not_equal, fill=1.0, base=0,
                                    pattern=[[-1, P]], channel_multiplier=1).then_inc(pool_consts, 1)
            pool.wait_ge(plan_step, 3)
            nc.gpsimd.partition_all_reduce(span_all, span, P, RMAX).then_inc(spans_reduced, 1)

            pool.wait_ge(plan_c_step, LIMITS)
            nc.gpsimd.partition_all_reduce(limits[:, 1], limits[:, 0], P, RMAX).then_inc(limits_reduced, 1)
            pool.wait_ge(plan_ready, 1)

            for k in range(3):
                pool.wait_ge(table_stored[k], 16 if k == 0 else 16 * NCH)

                def gather(g, n, r):
                    pool.wait_ge(indices_staged[k], g + 1)
                    pool.nop(nofuse=True)
                    for j in range(TILES):
                        pool.indirect_dma_start(
                            ring[:, r, j, :], None, tables[k],
                            bass.IndirectOffsetOnAxis(ap=staged[:, r, j:j + 1], axis=0),
                        ).then_inc(gathered[k][r], 16)

                def gather_some():
                    with pool.Fori(0, GATHERED // RING) as n:
                        for r in range(RING):
                            gather(n * RING + r, n, r)
                if k < 2:
                    either(pool, gather_some, lambda: over_groups(pool, gather))
                else:
                    over_groups(pool, gather)

        @block.scalar
        def _(act):
            def deviation(k):
                act.wait_ge(norm_step[k], 5)
                nc.scalar.activation(col_b[:], col_a[:], ACT.Sqrt, bias=eps[:], scale=1.0 / D)\
                    .then_inc(std_ready[k], 1)

            def sweep(k):
                if k:
                    act.wait_ge(sweep_done[k - 1], 1)
                nc.scalar.copy(staged[:].rearrange("p r t -> p (r t)"), flat(src_all)[:, 0:RING * TILES])\
                    .then_inc(indices_staged[k], RING)

                def body(g, n, r):
                    act.wait_ge(slot_free[k], g + 3)
                    act.nop(nofuse=True)
                    nc.scalar.copy(staged[:, r, :],
                                   flat(src_all)[:, bass.ds((g + RING) * TILES, TILES)])\
                        .then_inc(indices_staged[k], 1)
                    if k == 2:
                        act.wait_ge(msg_used, g + 1)
                        nc.scalar.activation(
                            msg[:, r % 2, :, 0:D], pre[:, r % 2, :].rearrange("p (t d) -> p t d", d=D),
                            ACT.Relu).then_inc(msg_ready, 1)

                def stage_indices(g, r):
                    act.wait_ge(scattered[k], g + 1)
                    act.nop(nofuse=True)
                    nc.scalar.copy(staged[:, r, :],
                                   flat(src_all)[:, bass.ds((g + RING) * TILES, TILES)])\
                        .then_inc(indices_staged[k], 1)

                def stage_keys(s, b):
                    if not isinstance(s, int) or s > 1:
                        act.wait_ge(marked[k], (s - 1) * (2 * TPS))
                        act.nop(nofuse=True)
                    nc.scalar.copy(keys_now[:, b].rearrange("p a t -> p (a t)"),
                                   keys[:, bass.ds(s, 1)].rearrange("p s a t -> p (s a t)"))\
                        .then_inc(keys_staged[k], 1)

                def supertile(s, b, n):
                    stage_keys(s + 1, 1 - b)
                    for t in range(TPS):
                        if t in ACT_TILES:
                            if t == 0 and not (isinstance(s, int) and s < 2):
                                act.wait_ge(applied[k], s - 1)
                            act.wait_ge(counted[k], s * TPS + t + 1)
                            nc.scalar.copy(slot_counts(b, t), tile_counts(t)).then_inc(copied_a[k], 1)
                        if t == 2 and not (isinstance(s, int) and s == 0):
                            stage_indices(s * 2 - 1, (2 * b - 1) % RING)
                        if t == 12:
                            stage_indices(s * 2, 2 * b)

                def narrow():
                    act.wait_ge(split_step[k], 7)
                    act.wait_ge(table_stored[k], 16 if k == 0 else 16 * NCH)
                    stage_keys(0, 0)
                    over_supertiles(act, supertile)
                    stage_indices(2 * NS - 1, RING - 1)
                    over_late_groups(act, lambda g, n, r: stage_indices(g, r))
                if k < 2:
                    either(act, narrow, lambda: over_groups(act, body))
                else:
                    over_groups(act, body)

            def stage_sums(k):
                act.wait_ge(sweep_done[k], 1)

                def body(c, b):
                    act.wait_ge(sums_turned[k], c + 1)
                    act.nop(nofuse=True)
                    nc.scalar.activation(stage_t[:, b, :], sums[0:D, bass.ds(c * CW, CW)],
                                         ACT.Relu if k == 0 else ACT.Copy).then_inc(sums_staged[k], 1)
                over_chunks(act, body)

            act.wait_ge(consts, 2)
            deviation(0)
            act.wait_ge(src_loaded, 16)
            act.wait_ge(pool_consts, 9)
            nc.scalar.copy(flat(src_all)[:, 0:NG * TILES], src_i).then_inc(src_narrowed, 1)
            act.wait_ge(src_narrowed, 1)
            act.wait_ge(plan_ready, 1)
            sweep(0)
            stage_sums(0)
            sweep(1)
            stage_sums(1)
            deviation(1)
            act.wait_ge(norm_step[1], 6)

            def stage_h(c, b):
                act.wait_ge(h_turned, c + 1)
                act.nop(nofuse=True)
                nc.scalar.copy(stage_r[:, b, :], flat(rows)[:, bass.ds(c * RW, RW)]).then_inc(h_staged, 1)
                act.wait_ge(h_turned, c + 3)
                act.wait_ge(projected, c + 1)
                nc.scalar.copy(h_t[:], psum[0:D, 0:CW]).then_inc(h_copied, 1)
            over_chunks(act, stage_h)
            act.sem_inc(msg_ready, 2)
            sweep(2)

            act.wait_ge(sweep_done[2], 1)

            def layer(c, b):
                act.wait_ge(l_turned, c + 1)
                act.nop(nofuse=True)
                nc.scalar.copy(stage_r[:, b, :], flat(rows)[:, bass.ds(c * RW, RW)]).then_inc(l_staged, 1)
                act.wait_ge(l_turned, c + 3)
                act.wait_ge(l_hidden, c + 1)
                nc.scalar.copy(h_t[:], bank(4, CW)[0:D, :]).then_inc(l_copied, 1)
                act.wait_ge(l_hidden, c + 2)
                act.wait_ge(l_out, c + 1)
                nc.scalar.activation(hid_t[0:D, :], bank(6, CW)[0:D, :], ACT.Relu, bias=b2a_col[:])\
                    .then_inc(l_relu, 1)
            over_chunks(act, layer)

        @block.tensor
        def _(pe):
            def scatter(k, g, values, width):
                first, count, before = group_plan(pe, g)
                with pe.Fori(0, count) as v:
                    pe.wait_ge(hit_built[k], before + v + 1)
                    pe.wait_ge(summed[k], before + v + 1)
                    pe.nop(nofuse=True)
                    for j in range(TILES):
                        mm = pe.matmul(bank(2, WINDOW)[0:width, :], values[:, j, 0:width], hit[:, j, :],
                                       start=(j == 0), stop=(j == TILES - 1))
                    mm.then_inc(scattered[k], 1)

            def by_banks(matmul):
                for a in range(0, CW, BANK):
                    mm = matmul(a, min(CW, a + BANK))
                return mm

            pe.wait_ge(weights_loaded, 16 * 11)
            pe.wait_ge(pool_consts, 9)
            pe.wait_ge(consts, 2)

            pe.wait_ge(plan_c_step, 1)
            for q in range(TPS):
                mm = pe.transpose(psum[0:NS, q * P:(q + 1) * P], dst_t[:, q * NS:(q + 1) * NS], ident[:])
            mm.then_inc(tiles_turned, 1)
            pe.wait_ge(plan_c_step, 4)
            for q in range(0, TPS, 4):
                cols = min(4, TPS - q) * NS
                mm = pe.matmul(bank(q // 4, cols), ones[0:NS, :], first_t[0:NS, q * NS:q * NS + cols],
                               start=True, stop=True)
            mm.then_inc(firsts_spread, 1)

            pe.wait_ge(plan_ready, 1)
            for k in range(2):
                def sum_rows(g, n, r):
                    pe.wait_ge(gathered[k][r], GROUP_LANDED * (n + 1))
                    scatter(k, g, ring[:, r], D)

                def place_group(g, n, r, sums_done):
                    pe.wait_ge(gathered[k][r], GROUP_LANDED * (n + 1))
                    pe.wait_ge(hit_built[k], g + 1)
                    pe.wait_ge(summed[k], sums_done)
                    pe.nop(nofuse=True)
                    for j in range(TILES):
                        mm = pe.matmul(bank(6, WINDOW)[0:D, :], ring[:, r, j, :], hit[:, j, :],
                                       start=(j == 0), stop=(j == TILES - 1))
                    mm.then_inc(scattered[k], 1)

                def place_supertile(s, sums_done):
                    pe.wait_ge(parts_ready[k], s * 2 + 2)
                    pe.wait_ge(summed[k], sums_done)
                    pe.nop(nofuse=True)
                    pe.matmul(bank(7, WIDE)[0:D, :], parts[:], hit_c[:], start=True, stop=True)\
                        .then_inc(placed[k], 1)

                def apply(s, b, a, z):
                    if a == 0:
                        tile_copied(pe, k, s, BY_VECTOR[-1])
                        tile_copied(pe, k, s, TPS - 1)
                        pe.nop(nofuse=True)
                    weights = counts[b].rearrange("p (s h) -> p s h", h=NT)
                    for c in range(a, z):
                        mm = pe.matmul(bank(4 + b, 3 * D), weights[:, :, c],
                                       thirds[:, c].rearrange("p a d -> p (a d)"),
                                       start=(c == 0), stop=(c == NT - 1))
                    if z == NT:
                        mm.then_inc(applied[k], 1)

                def supertile(s, b, n):
                    static = isinstance(s, int)
                    for t in range(TPS):
                        pe.wait_ge(marked[k], s * (2 * TPS) + 2 * t + 2)
                        if not static or s or t >= 2:
                            tile_copied(pe, k, s, t - 2)
                        pe.nop(nofuse=True)
                        slot = (b * TPS + t) % RING
                        for a in range(2):
                            mm = pe.matmul(bank(t % 2 * 2 + a, HK), low_ring[:, slot, :],
                                           key_ring[:, slot, a * HK:(a + 1) * HK], start=True, stop=True)
                        mm.then_inc(counted[k], 1)
                        if t >= 1 and not (static and s == 0):
                            apply(s - 1, 1 - b, NT * (t - 1) // (TPS - 1), NT * t // (TPS - 1))
                        if t == 3 and not (static and s < 2):
                            place_supertile(s - 2, sums_before(s) - 1)
                        if t == 8:
                            place_group(s * 2, n, 2 * b, sums_before(s) + (0 if static and s == 0 else 1))
                        if t == TPS - 1:
                            place_group(s * 2 + 1, n, 2 * b + 1,
                                        sums_before(s) + (1 if static and s == 0 else 2 if static else 3))

                def narrow():
                    pe.wait_ge(split_step[k], 7)
                    over_supertiles(pe, supertile)
                    total = sums_before(NS)
                    apply(NS - 1, 1, 0, NT)
                    place_supertile(NS - 2, total)
                    place_supertile(NS - 1, total + 2)
                    over_late_groups(pe, lambda g, n, r: place_group(g, n, r, g - 2 * NS + total + 3))
                either(pe, narrow, lambda: over_groups(pe, sum_rows))
                pe.sem_inc(sums_turned[k], 2)

                def turn(c, b):
                    pe.wait_ge(sums_staged[k], c + 1)
                    pe.wait_ge(sums_taken[k], c + 1)
                    pe.nop(nofuse=True)
                    for t in range(CHUNK):
                        mm = pe.transpose(bank(b)[:, t * D:(t + 1) * D], stage_t[:, b, t * P:(t + 1) * P],
                                          ident[0:D, 0:D])
                    mm.then_inc(sums_turned[k], 1)
                over_chunks(pe, turn)

            pe.sem_inc(h_turned, 2)
            pe.sem_inc(projected, 1)
            pe.sem_inc(h_copied, 1)

            def project(c, b):
                pe.wait_ge(h_staged, c + 1)
                pe.wait_ge(h_copied, c + 1)
                pe.nop(nofuse=True)
                for t in range(CHUNK):
                    mm = pe.transpose(psum[0:D, t * P:(t + 1) * P], stage_r[:, b, t * D:(t + 1) * D], ident[:])
                mm.then_inc(h_turned, 1)
                pe.wait_ge(h_copied, c + 2)
                pe.wait_ge(biased, c + 1)
                pe.nop(nofuse=True)
                for t in range(CHUNK):
                    mm = pe.matmul(bank(2 + b)[:, t * D:(t + 1) * D], h_t[:, t * P:(t + 1) * P], w_node[:],
                                   start=True, stop=True)
                mm.then_inc(projected, 1)
            over_chunks(pe, project)

            pe.wait_ge(late_consts, 1)
            pe.sem_inc(multiplied, RING)

            def messages(g, n, r):
                pe.wait_ge(attr_loaded[r], 16 * (n + 1))
                pe.wait_ge(slot_free[2], g + 1)
                for j in range(TILES // 2):
                    mm = pe.matmul(bank(r % 2)[:, j * P:(j + 1) * P],
                                   attr_ring[:, r, j * TILE:(j + 1) * TILE], w_attr[:], start=True, stop=True)
                mm.then_inc(multiplied, 1)
                pe.wait_ge(msg_ready, g + 3)
                scatter(2, g, msg[:, r % 2], D + 1)
            over_groups(pe, messages)

            pe.wait_ge(sweep_done[2], 1)
            pe.sem_inc(l_turned, 2)
            pe.sem_inc(l_hidden, 1)
            pe.sem_inc(l_out, 1)

            def layer(c, b):
                pe.wait_ge(l_rows, c + 1)
                pe.nop(nofuse=True)
                by_banks(lambda a, z: pe.matmul(psum[0:D, a:z], w1b_b[:], sums[:, bass.ds(c * CW + a, z - a)],
                                                start=True, stop=True))
                by_banks(lambda a, z: pe.matmul(psum[0:D, 2 * BANK + a:2 * BANK + z], count_all[:],
                                                sums[:, bass.ds(c * CW + a, z - a)],
                                                start=True, stop=True)).then_inc(l_means, 1)
                pe.wait_ge(l_staged, c + 1)
                pe.wait_ge(l_copied, c + 1)
                pe.nop(nofuse=True)
                for t in range(CHUNK):
                    mm = pe.transpose(bank(4, CW)[0:D, t * P:(t + 1) * P], stage_r[:, b, t * D:(t + 1) * D],
                                      ident[:])
                mm.then_inc(l_turned, 1)
                pe.wait_ge(l_copied, c + 2)
                pe.wait_ge(l_relu, c + 1)
                pe.nop(nofuse=True)
                by_banks(lambda a, z: pe.matmul(psum[0:D, 6 * BANK + a:6 * BANK + z], w2a_h[:], h_t[:, a:z],
                                                start=True, stop=False))
                pe.wait_ge(l_mean, c + 2)
                pe.nop(nofuse=True)
                by_banks(lambda a, z: pe.matmul(psum[0:D, 6 * BANK + a:6 * BANK + z], w2a_m[:], mean_t[:, a:z],
                                                start=False, stop=True)).then_inc(l_hidden, 1)
                pe.wait_ge(l_relu, c + 2)
                pe.nop(nofuse=True)
                for t in range(CHUNK):
                    mm = pe.matmul(bank(0)[:, t * D:(t + 1) * D], hid_t[:, t * P:(t + 1) * P], w2b_b[:],
                                   start=True, stop=True)
                mm.then_inc(l_out, 1)
            over_chunks(pe, layer)

        @block.vector
        def _(dve):
            def norm(k):
                rows3 = work.rearrange("p (t d) -> p t d", d=D)

                def spread(col):
                    return col[:].unsqueeze(2).to_broadcast([P, NT, D])

                nc.vector.tensor_reduce(col_a[:], x_rows[:], AX.X, ALU.add).then_inc(norm_step[k], 1)
                dve.wait_ge(norm_step[k], 1)
                nc.vector.tensor_scalar(col_b[:], col_a[:], 1.0 / D, None, ALU.mult).then_inc(norm_step[k], 1)
                dve.wait_ge(norm_step[k], 2)
                nc.vector.tensor_tensor(rows3, x_rows[:], spread(col_b), ALU.subtract)\
                    .then_inc(norm_step[k], 1)
                dve.wait_ge(norm_step[k], 3)
                nc.vector.tensor_tensor(flat(rows), work, work, ALU.mult).then_inc(norm_step[k], 1)
                dve.wait_ge(norm_step[k], 4)
                nc.vector.tensor_reduce(col_a[:], rows[:], AX.X, ALU.add).then_inc(norm_step[k], 1)
                dve.wait_ge(std_ready[k], 1)
                nc.vector.reciprocal(col_a[:], col_b[:]).then_inc(std_ready[k], 1)
                dve.wait_ge(std_ready[k], 2)
                nc.vector.scalar_tensor_tensor(out=rows[:], in0=rows3, scalar=0.0, in1=spread(col_a),
                                               op0=ALU.max, op1=ALU.mult).then_inc(norm_step[k], 1)

            nc.vector.memset(w_attr[:], 0.0).then_inc(consts, 1)
            nc.vector.memset(eps[:], EPS)
            nc.vector.memset(count_all[0:D, :], 0.0)
            nc.vector.memset(count_all[D:D + 1, :], 1.0)
            nc.vector.memset(limits[:, 0], 0.0)
            nc.vector.memset(ones[:], 1.0).then_inc(consts, 1)

            dve.wait_ge(x_loaded, 16)
            norm(0)

            dst_3 = dst_i.rearrange("p (g t) -> p g t", t=TILES)
            dve.wait_ge(dst_loaded, 16)
            nc.vector.tensor_reduce(span[:, 0:NG], dst_3, AX.X, ALU.max).then_inc(plan_step, 1)
            nc.vector.tensor_reduce(windows, dst_3, AX.X, ALU.min).then_inc(plan_step, 1)
            dve.wait_ge(plan_step, 2)
            nc.vector.tensor_scalar(span[:, NG:2 * NG], windows, -1.0, None, ALU.mult).then_inc(plan_step, 1)

            dve.wait_ge(dst_c_loaded, 16)
            nc.vector.tensor_copy(dst_t, dst_t.bitcast(I32)).then_inc(plan_c_step, 1)
            dve.wait_ge(tiles_turned, 1)
            turned = psum[0:NS, 0:TPS * P].rearrange("p (q e) -> p q e", e=P)
            nc.vector.tensor_reduce(col_min[0:NS, :], turned, AX.X, ALU.min).then_inc(plan_c_step, 1)
            nc.vector.tensor_reduce(col_max[0:NS, :], turned, AX.X, ALU.max).then_inc(plan_c_step, 1)
            dve.wait_ge(plan_c_step, 3)
            nc.vector.tensor_tensor(first_t[0:NS, :].rearrange("p (q m) -> p q m", q=TPS),
                                    ident[0:NS, 0:NS].unsqueeze(1).to_broadcast([NS, TPS, NS]),
                                    col_min[0:NS, :].unsqueeze(2).to_broadcast([NS, TPS, NS]), ALU.mult)\
                .then_inc(plan_c_step, 1)
            nc.vector.tensor_tensor(col_max[0:NS, :], col_max[0:NS, :], col_min[0:NS, :], ALU.subtract)\
                .then_inc(plan_c_step, 1)
            dve.wait_ge(plan_c_step, 5)
            nc.vector.tensor_reduce(limits[0:NS, 0, 0:1], col_max[0:NS, :], AX.X, ALU.max).then_inc(plan_c_step, 1)
            dve.wait_ge(pool_consts, 9)
            nc.vector.tensor_tensor(col_b[:, 0:TPS], mask[:], number[:, 0:TPS], ALU.mult).then_inc(plan_c_step, 1)
            dve.wait_ge(plan_c_step, 7)
            nc.vector.tensor_reduce(part_no[:], col_b[:, 0:TPS], AX.X, ALU.add).then_inc(plan_c_step, 1)
            dve.wait_ge(plan_c_step, 8)
            nc.vector.tensor_scalar(part_no[:], part_no[:], -float(SPAN), None, ALU.mult).then_inc(plan_c_step, 1)
            dve.wait_ge(plan_c_step, 9)
            nc.vector.tensor_tensor(part_no[:], part_no[:], tick_i[:], ALU.add).then_inc(plan_c_step, 1)
            dve.wait_ge(firsts_spread, 1)
            dve.wait_ge(plan_c_step, 10)
            for q in range(0, TPS, 4):
                cols = min(4, TPS - q) * NS
                nc.vector.tensor_copy(first_t[:, q * NS:q * NS + cols], bank(q // 4, cols))\
                    .then_inc(plan_c_step, 1)
            at = 10 + -(-TPS // 4)
            dve.wait_ge(plan_c_step, at)
            nc.vector.tensor_tensor(dst_t, dst_t, first_t, ALU.subtract).then_inc(plan_c_step, 1)
            dve.wait_ge(src_c_loaded, 16)
            keys_low, keys_high = keys[:, 0:NS, 0, :], keys[:, 0:NS, 1, :]
            nc.vector.tensor_scalar(work[:, 0:NC].bitcast(I32), src_t, P - 1, None, ALU.bitwise_and)\
                .then_inc(plan_c_step, 1)
            nc.vector.tensor_scalar(src_t, src_t, P.bit_length() - 1, None, ALU.logical_shift_right)\
                .then_inc(plan_c_step, 1)
            dve.wait_ge(plan_c_step, at + 3)
            nc.vector.tensor_copy(keys_low, work[:, 0:NC].bitcast(I32).rearrange("p (s t) -> p s t", t=TPS))\
                .then_inc(plan_c_step, 1)
            nc.vector.scalar_tensor_tensor(out=keys_high, in0=dst_t.rearrange("p (s t) -> p s t", t=TPS),
                                           scalar=float(NT), in1=src_t.rearrange("p (s t) -> p s t", t=TPS),
                                           op0=ALU.mult, op1=ALU.add).then_inc(plan_c_step, 1)
            firsts = first_t.rearrange("p (s t) -> p s t", t=TPS)
            nc.vector.tensor_tensor(work[:, NC:2 * NC].rearrange("p (s t) -> p s t", t=TPS), firsts,
                                    mask[:].unsqueeze(1).to_broadcast([P, NS, TPS]), ALU.mult)\
                .then_inc(plan_c_step, 1)
            nc.vector.tensor_copy(plan_c[0:1, :], firsts[0:1, :, 0]).then_inc(plan_c_step, 1)
            dve.wait_ge(plan_c_step, at + 7)
            nc.vector.tensor_reduce(slot_node[:], work[:, NC:2 * NC].rearrange("p (s t) -> p s t", t=TPS),
                                    AX.X, ALU.add).then_inc(plan_c_step, 1)
            dve.wait_ge(plan_c_step, at + 8)
            nc.vector.tensor_tensor(slot_node[:], slot_node[:], firsts[:, :, 0], ALU.subtract)\
                .then_inc(plan_c_step, 1)
            dve.wait_ge(plan_c_step, at + 9)
            nc.vector.tensor_scalar(slot_node[:], slot_node[:], part_no[:, 0:1], None, ALU.add)\
                .then_inc(plan_c_step, 1)
            dve.wait_ge(plan_c_step, at + 10)
            slots = TPS * SPAN
            nc.vector.tensor_reduce(limits[0:slots, 0, 1:2], slot_node[0:slots, :], AX.X, ALU.max)\
                .then_inc(plan_c_step, 1)
            nc.vector.tensor_reduce(limits[0:slots, 0, 2:3], slot_node[0:slots, :], AX.X, ALU.min)\
                .then_inc(plan_c_step, 1)
            dve.wait_ge(plan_c_step, at + 12)
            nc.vector.tensor_scalar(limits[0:slots, 0, 2:3], limits[0:slots, 0, 2:3], -1.0, None, ALU.mult)\
                .then_inc(plan_c_step, 1)

            dve.wait_ge(spans_reduced, 1)
            nc.vector.tensor_tensor(dst_rel[:], dst_3, minus_first.unsqueeze(2).to_broadcast([P, NG, TILES]),
                                    ALU.add).then_inc(plan_step, 1)
            nc.vector.tensor_tensor(windows_i, last, minus_first, ALU.add).then_inc(plan_step, 1)
            dve.wait_ge(plan_step, 5)
            nc.vector.tensor_scalar(windows_i, windows_i, SHIFT, None, ALU.logical_shift_right)\
                .then_inc(plan_step, 1)
            dve.wait_ge(plan_step, 6)
            nc.vector.tensor_scalar(windows, windows_i, 1.0, None, ALU.add).then_inc(plan_step, 1)
            dve.wait_ge(plan_step, 7)
            nc.vector.tensor_reduce(limits[:, 0, 3:4], windows[:, 0:GATHERED], AX.X, ALU.max)\
                .then_inc(plan_c_step, 1)
            nc.vector.memset(span[:, 0:NG], 1.0).then_inc(plan_step, 1)
            dve.wait_ge(plan_step, 8)
            nc.vector.tensor_tensor_scan(visits, span[:, 0:NG], windows, 0.0, ALU.mult, ALU.add)\
                .then_inc(plan_step, 1)
            dve.wait_ge(plan_step, 9)
            nc.vector.tensor_tensor(plan[0:1, :, 2], visits[0:1, :], windows[0:1, :], ALU.subtract)
            nc.vector.tensor_copy(plan[0:1, :, 1], windows[0:1, :])
            nc.vector.tensor_scalar(plan[0:1, :, 0], minus_first[0:1, :], -1.0, None, ALU.mult)\
                .then_inc(plan_step, 1)
            dve.wait_ge(limits_reduced, 1)
            for i, most in enumerate((SPAN - 1, WIDE - 1, 0, 1)):
                nc.vector.tensor_scalar(limits[:, 0, i:i + 1], limits[:, 1, i:i + 1], float(most), None,
                                        ALU.is_gt).then_inc(plan_step, 1)
            dve.wait_ge(plan_step, 14)
            nc.vector.tensor_reduce(wide[:], limits[:, 0, :], AX.X, ALU.max).then_inc(plan_step, 1)
            dve.wait_ge(plan_step, 15)
            dve.wait_ge(pool_consts, 9)
            nc.vector.memset(tick[:, 4:5], 0.0).then_inc(plan_ready, 1)

            def split(k):
                rest = work.rearrange("p (t d) -> p t d", d=D)
                step = split_step[k]
                dve.wait_ge(src_narrowed, 1)
                nc.vector.tensor_copy(thirds[:, :, 0, :], rows[:]).then_inc(step, 1)
                dve.wait_ge(step, 1)
                nc.vector.tensor_tensor(rest, rows[:], thirds[:, :, 0, :], ALU.subtract).then_inc(step, 1)
                dve.wait_ge(step, 2)
                nc.vector.tensor_copy(thirds[:, :, 1, :], rest).then_inc(step, 1)
                dve.wait_ge(step, 3)
                nc.vector.tensor_tensor(rest, rest, thirds[:, :, 1, :], ALU.subtract).then_inc(step, 1)
                dve.wait_ge(step, 4)
                nc.vector.tensor_copy(thirds[:, :, 2, :], rest).then_inc(step, 1)
                dve.wait_ge(step, 5)
                dve.wait_ge(table_stored[k], 16 if k == 0 else 16 * NCH)
                for b in range(2):
                    nc.vector.memset(counts[b][:, TPS * KEYS:P * NT], 0.0).then_inc(step, 1)

            def sweep(k):
                width = D if k < 2 else D + 1
                nc.vector.memset(arena[:], 0.0).then_inc(summed[k], 1)
                dve.sem_inc(slot_free[k], 2)
                dve.sem_inc(rel_step[k], 1)
                if k == 2:
                    dve.sem_inc(msg_used, 2)

                def window_at(begin, size):
                    begin = nc.s_assert_within(begin, 0, COLS - size,
                                               skip_runtime_bounds_check_because="spans end within the nodes")
                    return sums[0:width, bass.ds(begin, size)]

                def mark_hits(rel):
                    nc.vector.tensor_tensor(
                        hit[:], number[:, 0:WINDOW].unsqueeze(1).to_broadcast([P, TILES, WINDOW]),
                        rel.unsqueeze(2).to_broadcast([P, TILES, WINDOW]), ALU.is_equal).then_inc(hit_built[k], 1)

                def body(g, n, r):
                    first, count, before = group_plan(dve, g)
                    if k == 2:
                        dve.wait_ge(multiplied, g + 1 + RING)
                        dve.wait_ge(gathered[2][r], GROUP_LANDED * (n + 1))
                        dve.wait_ge(msg_ready, g + 1)
                        nc.vector.tensor_tensor(pre[:, r % 2, :], bank(r % 2),
                                                ring[:, r].rearrange("p t d -> p (t d)"), ALU.add)\
                            .then_inc(slot_free[2], 1)
                    dve.wait_ge(rel_step[k], before + g + 1)
                    dve.nop(nofuse=True)
                    nc.vector.tensor_copy(rel_now[:], dst_rel[:, bass.ds(g, 1), :].rearrange("p g t -> p (g t)"))\
                        .then_inc(rel_step[k], 1)
                    with dve.Fori(0, count) as v:
                        dve.wait_ge(rel_step[k], before + g + v + 2)
                        mark_hits(rel_now[:])
                        dve.wait_ge(hit_built[k], before + v + 1)
                        nc.vector.tensor_scalar(rel_now[:], rel_now[:], -float(WINDOW), None, ALU.add)\
                            .then_inc(rel_step[k], 1)
                        window = window_at(first + v * WINDOW, WINDOW)
                        dve.wait_ge(scattered[k], before + v + 1)
                        dve.wait_ge(summed[k], before + v + 1)
                        dve.nop(nofuse=True)
                        nc.vector.tensor_tensor(window, window, bank(2, WINDOW)[0:width, :], ALU.add)\
                            .then_inc(summed[k], 1)
                    nc.vector.memset(tick[:, 0:1], 0.0).then_inc(slot_free[k] if k < 2 else msg_used, 1)

                def mark_group(g):
                    mark_hits(dst_rel[:, bass.ds(g, 1), :].rearrange("p g t -> p (g t)"))

                def sum_group(g, sums_done):
                    first = dve.value_load(plan[0:1, bass.ds(g, 1), 0:1], min_val=0, max_val=n_nodes)
                    window = window_at(first, WINDOW)
                    dve.wait_ge(scattered[k], g + 1)
                    dve.wait_ge(summed[k], sums_done)
                    dve.nop(nofuse=True)
                    nc.vector.tensor_tensor(window, window, bank(6, WINDOW)[0:D, :], ALU.add)\
                        .then_inc(summed[k], 1)

                def add_parts(s, b):
                    dve.wait_ge(applied[k], s + 1)
                    dve.nop(nofuse=True)
                    nc.vector.tensor_reduce(parts[:], bank(4 + b, 3 * D).rearrange("p (a d) -> p d a", a=3),
                                            AX.X, ALU.add).then_inc(parts_ready[k], 1)
                    nc.vector.tensor_scalar(hit_c[:], number[:, 0:WIDE], slot_node[:, bass.ds(s, 1)], None,
                                            ALU.is_equal).then_inc(parts_ready[k], 1)

                def sum_supertile(s, sums_done):
                    first = dve.value_load(plan_c[0:1, bass.ds(s, 1)], min_val=0, max_val=n_nodes)
                    window = window_at(first, WIDE)
                    dve.wait_ge(placed[k], s + 1)
                    dve.wait_ge(summed[k], sums_done)
                    dve.nop(nofuse=True)
                    nc.vector.tensor_tensor(window, window, bank(7, WIDE)[0:D, :], ALU.add)\
                        .then_inc(summed[k], 1)

                def supertile(s, b, n):
                    static = isinstance(s, int)
                    dve.wait_ge(keys_staged[k], s + 1)
                    done = sums_before(s)
                    for t in range(TPS):
                        slot = (b * TPS + t) % RING
                        if not static or s or t >= RING:
                            dve.wait_ge(counted[k], s * TPS + (t - RING + 1))
                        nc.vector.tensor_scalar(low_ring[:, slot, :], number[:, 0:P], keys_now[:, b, 0, t:t + 1],
                                                None, ALU.is_equal).then_inc(marked[k], 1)
                        nc.vector.tensor_scalar(key_ring[:, slot, :], number[:], keys_now[:, b, 1, t:t + 1],
                                                None, ALU.is_equal).then_inc(marked[k], 1)
                        u = t - LAG
                        if u in BY_VECTOR:
                            if u == BY_VECTOR[0] and not (static and s < 2):
                                dve.wait_ge(applied[k], s - 1)
                            dve.wait_ge(counted[k], s * TPS + u + 1)
                            nc.vector.tensor_copy(slot_counts(b, u), tile_counts(u)).then_inc(copied_v[k], 1)
                        if t == 1 and not (static and s < 2):
                            add_parts(s - 2, b)
                        if t == 2 and not (static and s == 0):
                            sum_group(s * 2 - 1, done)
                            done = done + 1
                        if t == 4:
                            mark_group(s * 2)
                        if t == 7 and not (static and s < 2):
                            sum_supertile(s - 2, done)
                            done = done + 1
                        if t == 11:
                            sum_group(s * 2, done)
                            done = done + 1
                        if t == 13:
                            mark_group(s * 2 + 1)

                def late_group(g, n, r):
                    mark_group(g)
                    sum_group(g, g - 2 * NS + sums_before(NS) + 3)

                def narrow():
                    dve.sem_inc(copied_a[k], 1)
                    dve.sem_inc(copied_v[k], 1)
                    over_supertiles(dve, supertile)
                    total = sums_before(NS)
                    sum_group(2 * NS - 1, total)
                    add_parts(NS - 2, 0)
                    sum_supertile(NS - 2, total + 1)
                    add_parts(NS - 1, 1)
                    sum_supertile(NS - 1, total + 2)
                    over_late_groups(dve, late_group)

                if k < 2:
                    either(dve, narrow, lambda: over_groups(dve, body))
                else:
                    over_groups(dve, body)
                nc.vector.memset(tick[:, 1 + k:2 + k], 0.0).then_inc(sweep_done[k], 1)

            for k in range(2):
                if k:
                    dve.wait_ge(sums_staged[0], NCH)
                    dve.wait_ge(sums_taken[0], NCH + 2)
                split(k)
                dve.wait_ge(split_step[k], 7)
                sweep(k)
                if k:
                    dve.wait_ge(x_again, 16)
                dve.sem_inc(sums_taken[k], 2)

                def take(c, b):
                    dve.wait_ge(sums_turned[k], c + 3)
                    dve.nop(nofuse=True)
                    turned = bank(b, RW).rearrange("p (t d) -> p t d", d=D)
                    if k == 0:
                        nc.vector.tensor_copy(rows_at(rows, c), turned).then_inc(sums_taken[0], 1)
                    else:
                        nc.vector.tensor_tensor(rows_at(x_rows, c), rows_at(x_rows, c), turned, ALU.add)\
                            .then_inc(sums_taken[1], 1)
                over_chunks(dve, take)
            dve.wait_ge(sums_taken[1], NCH + 2)
            dve.wait_ge(table_stored[1], 16 * NCH)
            norm(1)
            dve.sem_inc(biased, 2)
            nc.vector.memset(hid_t[D:D + 1, :], 1.0)
            nc.vector.memset(msg[:, :, :, D:D + 1], 1.0).then_inc(late_consts, 1)

            def bias(c, b):
                dve.wait_ge(projected, c + 2)
                dve.nop(nofuse=True)
                nc.vector.tensor_tensor(rows_at(table_rows.rearrange("p (t d) -> p t d", d=D), c),
                                        bank(2 + b, RW).rearrange("p (t d) -> p t d", d=D),
                                        b1a_all[:].unsqueeze(1).to_broadcast([P, CHUNK, D]), ALU.add)\
                    .then_inc(biased, 1)
            over_chunks(dve, bias)
            dve.wait_ge(table_stored[2], 16 * NCH)
            sweep(2)

            dve.sem_inc(l_mean, 1)
            dve.sem_inc(l_rows, 1)
            dve.sem_inc(l_relu, 1)
            dve.sem_inc(l_copied, 1)

            def layer(c, b):
                dve.wait_ge(l_means, c + 1)
                dve.wait_ge(l_hidden, c + 1)
                nc.vector.tensor_scalar(inv_count, psum[0:D, 2 * BANK:2 * BANK + CW], 1.0, None, ALU.max)\
                    .then_inc(l_count, 1)
                dve.wait_ge(l_count, c * 2 + 1)
                nc.vector.reciprocal(inv_count, inv_count).then_inc(l_count, 1)
                dve.wait_ge(l_count, c * 2 + 2)
                nc.vector.tensor_tensor(mean_t, psum[0:D, 0:CW], inv_count, ALU.mult).then_inc(l_mean, 1)
                dve.wait_ge(l_out, c + 2)
                dve.nop(nofuse=True)
                nc.vector.tensor_tensor(rows_at(rows, c), bank(0, RW).rearrange("p (t d) -> p t d", d=D),
                                        rows_at(x_rows, c), ALU.add).then_inc(l_rows, 1)
            over_chunks(dve, layer)


def kernel(x, src, dst, edge_attr_64, L1_gnn_u, L1_gnn_w1a, L1_gnn_b1a, L1_gnn_w1b, L1_gnn_b1b,
           L1_gnn_w2a, L1_gnn_b2a, L1_gnn_w2b, L1_gnn_b2b):
    import numpy as _np
    import concourse.bacc as _bacc
    from concourse import mybir as _mybir
    from concourse.bass_utils import run_bass_kernel_spmd as _run

    n_nodes, d = x.shape
    n_edges = src.shape[0]
    node_rows = -(-n_nodes // (P * CHUNK)) * P * CHUNK
    groups = -(-n_edges // (TILE * TILES))
    n_pad = groups * TILE * TILES - n_edges

    def by_partition(index, fill):
        a = _np.concatenate([_np.asarray(index), _np.full(n_pad, fill, _np.asarray(index).dtype)])
        return _np.ascontiguousarray(a.reshape(groups, TILE, TILES).transpose(1, 0, 2).reshape(TILE, -1))

    def by_tile(index, fill):
        a = _np.concatenate([_np.asarray(index), _np.full(n_pad, fill, _np.asarray(index).dtype)])
        return _np.ascontiguousarray(a.reshape(-1, TILE)[GATHERED * TILES:].T)

    attr = _np.concatenate([_np.asarray(edge_attr_64), _np.zeros((n_pad, d), _np.float32)])
    attr = attr.reshape(groups, TILE, TILES // 2, 2, d).transpose(0, 3, 4, 2, 1)
    arrays = {
        "x": _np.concatenate([_np.asarray(x), _np.zeros((node_rows - n_nodes, d), _np.float32)]),
        "src": by_partition(src, 0),
        "dst": by_partition(dst, n_nodes),
        "src_c": by_tile(src, 0),
        "dst_c": by_tile(dst, n_nodes),
        "attr": _np.ascontiguousarray(attr.reshape(groups, 2 * d, TILES // 2 * TILE)),
        "w1a": L1_gnn_w1a, "b1a": L1_gnn_b1a, "w1b": L1_gnn_w1b, "b1b": L1_gnn_b1b,
        "w2a": L1_gnn_w2a, "b2a": L1_gnn_b2a, "w2b": L1_gnn_w2b, "b2b": L1_gnn_b2b,
    }
    arrays = {n: _np.ascontiguousarray(a) for n, a in arrays.items()}
    nc = _bacc.Bacc("TRN2", target_bir_lowering=False, num_devices=1)
    args = [nc.dram_tensor(f"in_{n}", a.shape, _mybir.dt.from_np(a.dtype), kind="ExternalInput").ap()
            for n, a in arrays.items()]
    out = nc.dram_tensor("out_0", (n_nodes, d), _mybir.dt.float32, kind="ExternalOutput").ap()
    gnn_kernel(nc, *args, out)
    r = _run(nc, [{f"in_{n}": a for n, a in arrays.items()}], core_ids=[0])
    return r.results[0]["out_0"]
```

```python
from contextlib import ExitStack

import concourse.bass as bass
from concourse import mybir

P = 128
TILE = 128
TILES = 8
RING = 4
WINDOW = 64
SPAN = 6
TPS = 21
WIDE = 96
GATHERED = 178
MARKS = 6
LAG = 3
BY_VECTOR = (9,)
CHUNK = 7
EPS = 1e-5

ALU = mybir.AluOpType
ACT = mybir.ActivationFunctionType
F32 = mybir.dt.float32
I32 = mybir.dt.int32
I16 = mybir.dt.int16
BF16 = mybir.dt.bfloat16
U32 = mybir.dt.uint32
AX = mybir.AxisListType
RMAX = bass.bass_isa.ReduceOp.max


def gnn_kernel(nc, x, src, dst, src_c, dst_c, attr, w1a, b1a, w1b, b1b, w2a, b2a, w2b, b2b, out):
    n_nodes, D = out.shape
    NT = x.shape[0] // P
    NCH = NT // CHUNK
    NG = attr.shape[0]
    CW = CHUNK * P
    RW = CHUNK * D
    BANK = 512
    COLS = NT * P + WINDOW
    GROUP_LANDED = 16 * TILES
    SHIFT = WINDOW.bit_length() - 1
    FULL = n_nodes // P
    REST = n_nodes - FULL * P
    assert NCH * CHUNK == NT and NCH % 2 == 0 and TILES * D <= BANK and RW <= BANK and CW <= 2 * BANK
    NC = src_c.shape[1]
    NS = NC // TPS
    KEYS = SPAN * NT
    HK = KEYS // 2
    ACT_TILES = [t for t in range(TPS) if t not in BY_VECTOR]
    assert NS * TPS == NC and NS % 2 == 0 and NS > 4 and GATHERED >= 2 * NS
    assert GATHERED * TILES + NC >= NG * TILES and HK * 2 == KEYS and HK <= BANK and TPS * SPAN <= P
    assert RING == 4 and 2 * TPS % MARKS == 0 and NS <= P
    assert n_nodes < NT * P and WINDOW == 1 << SHIFT and NG % RING and TILE == P

    with ExitStack() as ctx:
        def sb(name, shape, dt=F32):
            return ctx.enter_context(nc.sbuf_tensor(name, shape, dt))

        def sem(name):
            return ctx.enter_context(nc.semaphore(name))

        STORES = (2, NCH, NCH)
        tables = [nc.dram_tensor(f"table{k}", [NT * P, D], F32).ap() for k in range(3)]
        psum = ctx.enter_context(nc.psum_tensor("psum", [P, 8 * BANK], F32))

        def bank(b, width=BANK):
            return psum[:, b * BANK:b * BANK + width]

        src_all = sb("src_all", [P, NG + RING, TILES], I16)
        dst_rel = sb("dst_rel", [P, NG, TILES], I16)
        plan = sb("plan", [P, NG, 3], I32)
        number = sb("number", [P, KEYS], I16)
        staged = sb("staged", [P, RING, TILES], U32)
        ring = sb("ring", [P, RING, TILES, D])
        rel_now = sb("rel_now", [P, TILES])
        hit = sb("hit", [P, TILES, WINDOW])
        tick = sb("tick", [P, 5])
        tick_i = sb("tick_i", [P, 1], I32)

        keys = sb("keys", [P, NS + 1, 2, TPS])
        keys_now = sb("keys_now", [P, 2, 2, TPS])
        low_ring = sb("low_ring", [P, MARKS, P], BF16)
        key_ring = sb("key_ring", [P, MARKS, KEYS], BF16)
        slot_node = sb("slot_node", [P, NS])
        plan_c = sb("plan_c", [P, NS], I32)
        wide = sb("wide", [P, 1], I32)
        parts = sb("parts", [P, D])
        hit_c = sb("hit_c", [P, WIDE])
        mask = sb("mask", [P, TPS])
        part_no = sb("part_no", [P, 1])
        ones = sb("ones", [P, P])
        limits = sb("limits", [P, 2, 4])
        col_min = sb("col_min", [P, TPS])
        col_max = sb("col_max", [P, TPS])

        x_rows = sb("x_rows", [P, NT, D])
        rows = sb("rows", [P, NT, D])
        arena = sb("arena", [P, COLS])
        thirds = sb("thirds", [P, NT, 3, D], BF16)
        col_a = sb("col_a", [P, NT])
        col_b = sb("col_b", [P, NT])
        stage_t = sb("stage_t", [D + 1, 2, CW])
        counts = [flat_[:].rearrange("p t d -> p (t d)").bitcast(BF16) for flat_ in (rows, x_rows)]

        thirds_f = thirds[:].rearrange("p t a d -> p (t a d)").bitcast(F32)
        used = [0]

        def in_thirds(n, partitions=P):
            used[0] += n
            assert used[0] <= NT * 3 * D // 2
            return thirds_f[0:partitions, used[0] - n:used[0]]

        src_i = in_thirds(NG * TILES).bitcast(I32)
        dst_t = in_thirds(NC)
        src_t = in_thirds(NC).bitcast(I32)
        first_t = in_thirds(NC)
        used[0] = 0
        table_rows = in_thirds(NT * D).rearrange("p (t d) -> p t d", d=D)
        stage_r = in_thirds(2 * RW).rearrange("p (b e) -> p b e", b=2)
        h_t = in_thirds(CW, D + 1)
        hid_t = h_t
        used[0] = 0
        attr_ring = in_thirds(RING * TILES // 2 * TILE).rearrange("p (r e) -> p r e", r=RING)
        pre = in_thirds(2 * TILES * D).rearrange("p (b e) -> p b e", b=2)
        msg = in_thirds(2 * TILES * (D + 1)).rearrange("p (b t d) -> p b t d", b=2, t=TILES)

        sums = arena[0:D + 1, :]
        work = arena[:, 0:NT * D]
        rows_work = work.rearrange("p (t d) -> p t d", d=D)
        LIMITS = 24 + -(-TPS // 4)
        THIRDS_FREE = LIMITS - 5
        ring_flat = ring[:].rearrange("p r t d -> p (r t d)")
        centred = [ring_flat[:, b * RW:(b + 1) * RW].rearrange("p (t d) -> p t d", d=D) for b in range(2)]
        squares = [ring_flat[:, (2 + b) * RW:(3 + b) * RW].rearrange("p (t d) -> p t d", d=D) for b in range(2)]
        col_n = sb("col_n", [P, 2, 4, CHUNK])
        at_ = [NT * D]

        def scratch(n):
            at_[0] += n
            return arena[:, at_[0] - n:at_[0]]

        dst_i = scratch(NG * TILES).bitcast(I32)
        span = scratch(2 * NG)
        span_all = scratch(2 * NG)
        windows_i = scratch(NG).bitcast(I32)
        windows = scratch(NG)
        visits = scratch(NG)
        assert at_[0] <= COLS
        last, minus_first = span_all[:, 0:NG], span_all[:, NG:2 * NG]

        ident = sb("ident", [P, P])
        eps = sb("eps", [P, 1])
        w_attr = sb("w_attr", [P, 2 * D])
        w_node = sb("w_node", [D + 1, 2 * D])
        w1b_b = sb("w1b_b", [D + 1, D])
        w1b_t = sb("w1b_t", [D, D + 1])
        w2a_m = sb("w2a_m", [D, D])
        w_sums = sb("w_sums", [D + 1, D + 1])
        w2b_b = sb("w2b_b", [D + 1, D])

        dst_loaded = sem("dst_loaded")
        x_loaded = [sem(f"x_loaded{h}") for h in range(2)]
        src_loaded = sem("src_loaded")
        src_narrowed = sem("src_narrowed")
        weights_loaded = sem("weights_loaded")
        pool_consts = sem("pool_consts")
        consts = sem("consts")
        plan_step = sem("plan_step")
        spans_reduced = sem("spans_reduced")
        plan_ready = sem("plan_ready")
        norm_step = sem("norm_step")
        squared = sem("squared")
        deviation_ready = sem("deviation_ready")
        inverted = sem("inverted")
        table_stored = [sem(f"table_stored{k}") for k in range(3)]
        plan_c_step = sem("plan_c_step")
        tiles_turned = sem("tiles_turned")
        firsts_spread = sem("firsts_spread")
        limits_reduced = sem("limits_reduced")
        src_c_loaded = sem("src_c_loaded")
        dst_c_loaded = sem("dst_c_loaded")
        x_again = [sem(f"x_again{b}") for b in range(2)]
        late_consts = sem("late_consts")
        part_cast = [sem(f"part_cast{k}") for k in range(2)]
        split_step = [sem(f"split_step{k}") for k in range(2)]
        sweep_done = [sem(f"sweep_done{k}") for k in range(3)]
        rel_step = [sem(f"rel_step{k}") for k in range(3)]
        keys_staged = [sem(f"keys_staged{k}") for k in range(2)]
        marked = [sem(f"marked{k}") for k in range(2)]
        counted = [sem(f"counted{k}") for k in range(2)]
        copied_a = [sem(f"copied_a{k}") for k in range(2)]
        copied_v = [sem(f"copied_v{k}") for k in range(2)]
        applied = [sem(f"applied{k}") for k in range(2)]
        parts_ready = [sem(f"parts_ready{k}") for k in range(2)]
        placed = [sem(f"placed{k}") for k in range(2)]
        indices_staged = [sem(f"indices_staged{k}") for k in range(3)]
        gathered = [[sem(f"gathered{k}_{r}") for r in range(RING)] for k in range(3)]
        slot_free = [sem(f"slot_free{k}") for k in range(3)]
        hit_built = [sem(f"hit_built{k}") for k in range(3)]
        scattered = [sem(f"scattered{k}") for k in range(3)]
        summed = [sem(f"summed{k}") for k in range(3)]
        attr_loaded = [sem(f"attr_loaded{r}") for r in range(RING)]
        multiplied = sem("multiplied")
        msg_ready = sem("msg_ready")
        msg_used = sem("msg_used")
        sums_staged = sem("sums_staged")
        sums_turned = sem("sums_turned")
        sums_taken = sem("sums_taken")
        m_staged = sem("m_staged")
        m_turned = sem("m_turned")
        m_centred = sem("m_centred")
        m_squared = sem("m_squared")
        m_summed = sem("m_summed")
        m_deviation = sem("m_deviation")
        m_h = sem("m_h")
        m_h_turned = sem("m_h_turned")
        m_h_copied = sem("m_h_copied")
        m_projected = sem("m_projected")
        m_table = sem("m_table")
        m_hidden = sem("m_hidden")
        l_staged = sem("l_staged")
        l_product = sem("l_product")
        l_mean = sem("l_mean")
        l_relu = sem("l_relu")
        l_turned = sem("l_turned")
        l_copied = sem("l_copied")
        l_out = sem("l_out")
        l_rows = sem("l_rows")
        weights_made = sem("weights_made")
        weights_step = sem("weights_step")
        stored = sem("stored")

        def over_groups(eng, body):
            with eng.Fori(0, NG // RING) as n:
                for r in range(RING):
                    body(n * RING + r, n, r)
            for r in range(NG % RING):
                body(NG // RING * RING + r, NG // RING, r)

        def over_chunks(eng, body):
            with eng.Fori(0, NCH // 2) as n:
                for b in range(2):
                    body(n * 2 + b, b)

        def over_steps(eng, step):
            for i in range(2):
                step(i, i)
            with eng.Fori(1, NCH // 2 - 1) as n:
                for b in range(2):
                    step(n * 2 + b, b)
            for i in range(NCH - 2, NCH + 2):
                step(i, i % 2)

        def chunk_in(i, c):
            return not isinstance(i, int) or 0 <= c < NCH

        def after(eng, done, count):
            if not isinstance(count, int) or count > 0:
                eng.wait_ge(done, count)

        def projected():
            return bank(4, CW).rearrange("p (t e) -> p t e", t=CHUNK)

        def group_plan(eng, g):
            first = eng.value_load(plan[0:1, bass.ds(g, 1), 0:1], min_val=0, max_val=n_nodes)
            count = eng.value_load(plan[0:1, bass.ds(g, 1), 1:2], min_val=1, max_val=n_nodes // WINDOW + 1)
            before = eng.value_load(plan[0:1, bass.ds(g, 1), 2:3], min_val=0,
                                    max_val=NG * (n_nodes // WINDOW + 1))
            return first, count, before

        def tile_copied(eng, k, s, t):
            if t < 0:
                s, t = s - 1, t + TPS
            if t in BY_VECTOR:
                eng.wait_ge(copied_v[k], s * len(BY_VECTOR) + BY_VECTOR.index(t) + 2)
            else:
                eng.wait_ge(copied_a[k], s * len(ACT_TILES) + ACT_TILES.index(t) + 2)

        def sums_before(s):
            return s * 3 - 2 if not isinstance(s, int) or s > 1 else s + 1

        def first_bank(b, t):
            return (b * TPS + t) % 2 * 2

        def tile_counts(b, t):
            return psum[:, first_bank(b, t) * BANK:(first_bank(b, t) + 2) * BANK].rearrange("p (a e) -> p a e", a=2)[:, :, 0:HK]

        def slot_counts(b, t):
            return counts[b][:, t * KEYS:(t + 1) * KEYS].rearrange("p (a e) -> p a e", a=2)

        def over_supertiles(eng, body):
            for b in range(2):
                body(b, b, 0)
            with eng.Fori(1, NS // 2) as n:
                for b in range(2):
                    body(n * 2 + b, b, n)

        def over_late_groups(eng, body):
            with eng.Fori(NS // 2, GATHERED // RING) as n:
                for r in range(RING):
                    body(n * RING + r, n, r)
            for r in range(GATHERED % RING):
                body(GATHERED // RING * RING + r, GATHERED // RING, r)
            assert NS // 2 < GATHERED // RING

        def either(eng, narrow, gather_all):
            flag = eng.value_load(wide[0:1, 0:1], min_val=0, max_val=1)
            with eng.If(flag == 0):
                narrow()
            with eng.Else():
                gather_all()

        def tiled(dram):
            return dram.rearrange("(t p) d -> p t d", p=P)

        def chunk_of(dram, c):
            return dram.rearrange("(c t p) d -> c p t d", p=P, t=CHUNK)[bass.ds(c, 1)]\
                .rearrange("c p t d -> (c p) t d")

        def half_of(dram, h):
            return tiled(dram)[:, h * (NT // 2):(h + 1) * (NT // 2)]

        def half(buffer, h):
            return buffer[:, h * (NT // 2):(h + 1) * (NT // 2)]

        def rows_at(buffer, c):
            return buffer[:, bass.ds(c * CHUNK, CHUNK), :]

        def flat(buffer):
            return buffer[:].rearrange("p t d -> p (t d)")

        block = ctx.enter_context(nc.Block())

        @block.sync
        def _(sp):
            sp.dma_start(dst_i, dst).then_inc(dst_loaded, 16)
            sp.dma_start(dst_t.bitcast(I32), dst_c).then_inc(dst_c_loaded, 16)
            for h in range(2):
                sp.dma_start(half(x_rows, h), half_of(x, h)).then_inc(x_loaded[h], 16)
            sp.dma_start(src_t, src_c).then_inc(src_c_loaded, 16)
            sp.dma_start(src_i, src).then_inc(src_loaded, 16)
            sp.wait_ge(consts, 1)
            for here, there in (
                (w_attr[0:D, 0:D], w1a[D:2 * D, :]), (w_attr[D:2 * D, D:2 * D], w1a[D:2 * D, :]),
                (w_node[0:D, 0:D], w1a[0:D, :]), (w_node[D:D + 1, 0:D], b1a.rearrange("(a d) -> a d", a=1)),
                (w_node[0:D, D:2 * D], w2a[0:D, :]), (w_node[D:D + 1, D:2 * D], b2a.rearrange("(a d) -> a d", a=1)),
                (w1b_b[0:D, :], w1b), (w1b_b[D:D + 1, :], b1b.rearrange("(a d) -> a d", a=1)),
                (w2a_m[:], w2a[D:2 * D, :]),
                (w2b_b[0:D, :], w2b), (w2b_b[D:D + 1, :], b2b.rearrange("(a d) -> a d", a=1)),
            ):
                sp.dma_start(here, there).then_inc(weights_loaded, 16)

            for h in range(2):
                sp.wait_ge(norm_step, 9 + h)
                sp.dma_start(half_of(tables[0], h), half(rows, h)).then_inc(table_stored[0], 16)
            with sp.Fori(0, NCH) as c:
                sp.wait_ge(sums_taken, c + 3)
                sp.dma_start(chunk_of(tables[1], c), rows_at(rows, c)).then_inc(table_stored[1], 16)
            sp.wait_ge(sweep_done[1], 1)
            def load_x(c, b):
                sp.dma_start(rows_at(x_rows, c), chunk_of(x, c)).then_inc(x_again[b], 16)
            for b in range(2):
                load_x(b, b)
            with sp.Fori(1, NCH // 2) as n:
                for b in range(2):
                    sp.wait_ge(m_centred, n * 8 + b * 4 - 7)
                    load_x(n * 2 + b, b)
            with sp.Fori(0, NCH) as c:
                sp.wait_ge(m_table, c + 1)
                sp.dma_start(chunk_of(tables[2], c), rows_at(table_rows, c)).then_inc(table_stored[2], 16)
            sp.wait_ge(table_stored[2], 16 * NCH)

            def load_attr(g, n, r):
                sp.wait_ge(multiplied, g + 1)
                sp.dma_start(attr_ring[:, r, :], attr[bass.ds(g, 1)].rearrange("g p e -> (g p) e"))\
                    .then_inc(attr_loaded[r], 16)
            over_groups(sp, load_attr)

            whole = FULL // CHUNK
            with sp.Fori(0, whole) as c:
                sp.wait_ge(l_rows, c + 1)
                sp.dma_start(chunk_of(out[0:whole * CHUNK * P, :], c), rows_at(rows, c)).then_inc(stored, 16)
            sp.wait_ge(l_rows, NCH)
            if FULL > whole * CHUNK:
                sp.dma_start(tiled(out[whole * CHUNK * P:FULL * P, :]), rows[:, whole * CHUNK:FULL, :])\
                    .then_inc(stored, 16)
            if REST:
                sp.dma_start(out[FULL * P:n_nodes, :], rows[0:REST, FULL, :]).then_inc(stored, 16)
            sp.wait_ge(stored, 16 * (whole + (FULL > whole * CHUNK) + (REST > 0)))

        @block.gpsimd
        def _(pool):
            nc.gpsimd.memset(ident[:], 0.0).then_inc(pool_consts, 1)
            nc.gpsimd.memset(flat(src_all)[:, NG * TILES:], 0).then_inc(pool_consts, 1)
            nc.gpsimd.memset(keys[:, NS], 0.0).then_inc(pool_consts, 1)
            nc.gpsimd.memset(mask[:], 1.0).then_inc(pool_consts, 1)
            nc.gpsimd.iota(number[:], pattern=[[1, KEYS]], base=0, channel_multiplier=0).then_inc(pool_consts, 1)
            nc.gpsimd.iota(tick_i[:], pattern=[[0, 1]], base=0, channel_multiplier=1).then_inc(pool_consts, 1)
            pool.wait_ge(pool_consts, 6)
            nc.gpsimd.affine_select(out=mask[:], in_=mask[:], compare_op=ALU.is_ge, fill=0.0, base=0,
                                    pattern=[[-SPAN, TPS]], channel_multiplier=1).then_inc(pool_consts, 1)
            pool.wait_ge(pool_consts, 7)
            nc.gpsimd.affine_select(out=mask[:], in_=mask[:], compare_op=ALU.is_ge, fill=0.0, base=SPAN - 1,
                                    pattern=[[SPAN, TPS]], channel_multiplier=-1).then_inc(pool_consts, 1)
            nc.gpsimd.affine_select(out=ident[:], in_=ident[:], compare_op=ALU.not_equal, fill=1.0, base=0,
                                    pattern=[[-1, P]], channel_multiplier=1).then_inc(pool_consts, 1)
            pool.wait_ge(plan_step, 3)
            nc.gpsimd.partition_all_reduce(span_all, span, P, RMAX).then_inc(spans_reduced, 1)

            pool.wait_ge(plan_c_step, LIMITS)
            nc.gpsimd.partition_all_reduce(limits[:, 1], limits[:, 0], P, RMAX).then_inc(limits_reduced, 1)

            for k in range(3):
                pool.wait_ge(table_stored[k], 16 * STORES[k])

                def gather(g, n, r):
                    pool.wait_ge(indices_staged[k], g + 1)
                    pool.nop(nofuse=True)
                    for j in range(TILES):
                        pool.indirect_dma_start(
                            ring[:, r, j, :], None, tables[k],
                            bass.IndirectOffsetOnAxis(ap=staged[:, r, j:j + 1], axis=0),
                        ).then_inc(gathered[k][r], 16)

                def gather_up_to(groups):
                    with pool.Fori(1, groups // RING) as n:
                        for r in range(RING):
                            gather(n * RING + r, n, r)
                    for r in range(groups % RING):
                        gather(groups // RING * RING + r, groups // RING, r)

                for r in range(RING):
                    gather(r, 0, r)
                if k == 0:
                    pool.wait_ge(plan_ready, 1)
                if k < 2:
                    either(pool, lambda: gather_up_to(GATHERED), lambda: gather_up_to(NG))
                else:
                    gather_up_to(NG)

        @block.scalar
        def _(act):
            def norm():
                for h in range(2):
                    act.wait_ge(norm_step, h * 3 + 3)
                    nc.scalar.activation(half(rows, h), half(rows_work, h), ACT.Square).then_inc(squared, 1)
                for h in range(2):
                    act.wait_ge(norm_step, 7 + h)
                    nc.scalar.activation(half(col_b, h), half(col_a, h), ACT.Sqrt, bias=eps[:], scale=1.0 / D)\
                        .then_inc(deviation_ready, 1)

            def split(k):
                for part in range(3):
                    for h in range(2):
                        if part == 0 and k == 0:
                            act.wait_ge(norm_step, 9 + h)
                        if part:
                            act.wait_ge(split_step[k], part * 2 - 1 + h)
                        nc.scalar.copy(half(thirds, h)[:, :, part, :], half(rows if part == 0 else rows_work, h))\
                            .then_inc(part_cast[k], 1)

            def stage_first_indices(k):
                nc.scalar.copy(staged[:].rearrange("p r t -> p (r t)"), flat(src_all)[:, 0:RING * TILES])\
                    .then_inc(indices_staged[k], RING)

            def sweep(k):
                def body(g, n, r):
                    act.wait_ge(slot_free[k], g + 3)
                    act.nop(nofuse=True)
                    nc.scalar.copy(staged[:, r, :],
                                   flat(src_all)[:, bass.ds((g + RING) * TILES, TILES)])\
                        .then_inc(indices_staged[k], 1)
                    if k == 2:
                        act.wait_ge(msg_used, g + 1)
                        nc.scalar.activation(
                            msg[:, r % 2, :, 0:D], pre[:, r % 2, :].rearrange("p (t d) -> p t d", d=D),
                            ACT.Relu).then_inc(msg_ready, 1)

                def stage_indices(g, r):
                    act.wait_ge(scattered[k], g + 1)
                    act.nop(nofuse=True)
                    nc.scalar.copy(staged[:, r, :],
                                   flat(src_all)[:, bass.ds((g + RING) * TILES, TILES)])\
                        .then_inc(indices_staged[k], 1)

                def stage_keys(s, b):
                    if not isinstance(s, int) or s > 1:
                        act.wait_ge(marked[k], (s - 1) * (2 * TPS))
                        act.nop(nofuse=True)
                    nc.scalar.copy(keys_now[:, b].rearrange("p a t -> p (a t)"),
                                   keys[:, bass.ds(s, 1)].rearrange("p s a t -> p (s a t)"))\
                        .then_inc(keys_staged[k], 1)

                def supertile(s, b, n):
                    stage_keys(s + 1, 1 - b)
                    for t in range(TPS):
                        if t in ACT_TILES:
                            if t == 0 and not (isinstance(s, int) and s < 2):
                                act.wait_ge(applied[k], s - 1)
                            act.wait_ge(counted[k], s * TPS + t + 1)
                            nc.scalar.copy(slot_counts(b, t), tile_counts(b, t)).then_inc(copied_a[k], 1)
                        if t == 2 and not (isinstance(s, int) and s == 0):
                            stage_indices(s * 2 - 1, (2 * b - 1) % RING)
                        if t == 12:
                            stage_indices(s * 2, 2 * b)

                def narrow():
                    act.wait_ge(split_step[k], 7)
                    act.wait_ge(table_stored[k], 16 * STORES[k])
                    stage_keys(0, 0)
                    over_supertiles(act, supertile)
                    stage_indices(2 * NS - 1, RING - 1)
                    over_late_groups(act, lambda g, n, r: stage_indices(g, r))
                    act.wait_ge(indices_staged[k], GATHERED + RING)

                def gather_all():
                    over_groups(act, body)
                    act.wait_ge(indices_staged[k], NG + RING)

                if k < 2:
                    either(act, narrow, gather_all)
                else:
                    over_groups(act, body)

            def stage_sums(c, b):
                act.wait_ge(sums_turned, c + 1)
                act.nop(nofuse=True)
                nc.scalar.activation(stage_t[0:D, b, :], sums[0:D, bass.ds(c * CW, CW)],
                                     ACT.Relu).then_inc(sums_staged, 1)

            def norm_and_project(i, b):
                if chunk_in(i, i + 1):
                    stage_x(i + 1, 1 - b)
                if chunk_in(i, i - 1):
                    act.wait_ge(m_centred, i * 4)
                    nc.scalar.activation(squares[1 - b], centred[1 - b], ACT.Square).then_inc(m_squared, 1)
                if chunk_in(i, i - 2):
                    act.wait_ge(m_h_turned, i - 1)
                    after(act, m_projected, i - 2)
                    nc.scalar.copy(h_t[0:D, :], bank(2, CW)[0:D, :]).then_inc(m_h_copied, 1)
                if chunk_in(i, i - 1):
                    act.wait_ge(m_summed, i)
                    nc.scalar.activation(col_n[:, 1 - b, 3, :], col_n[:, 1 - b, 2, :], ACT.Sqrt, bias=eps[:],
                                         scale=1.0 / D).then_inc(m_deviation, 1)
                if chunk_in(i, i - 2):
                    act.wait_ge(m_projected, i - 1)
                    act.nop(nofuse=True)
                    nc.scalar.copy(rows_at(table_rows, i - 2), projected()[:, :, 0:D]).then_inc(m_table, 1)

            def stage_x(c, b):
                after(act, m_turned, c - 1)
                act.nop(nofuse=True)
                nc.scalar.copy(stage_t[0:D, b, :], sums[0:D, bass.ds(c * CW, CW)]).then_inc(m_staged, 1)

            act.wait_ge(consts, 2)
            norm()
            act.wait_ge(src_loaded, 16)
            act.wait_ge(pool_consts, 9)
            nc.scalar.copy(flat(src_all)[:, 0:NG * TILES], src_i).then_inc(src_narrowed, 1)
            act.wait_ge(src_narrowed, 1)
            stage_first_indices(0)
            act.wait_ge(plan_c_step, THIRDS_FREE)
            split(0)
            act.wait_ge(plan_ready, 1)
            sweep(0)
            act.wait_ge(sweep_done[0], 1)
            stage_first_indices(1)
            over_chunks(act, stage_sums)
            act.wait_ge(sums_taken, NCH + 2)
            split(1)
            sweep(1)
            act.wait_ge(sweep_done[1], 1)
            stage_first_indices(2)
            stage_x(0, 0)
            over_steps(act, norm_and_project)
            act.sem_inc(msg_ready, 2)
            act.wait_ge(late_consts, 2)
            sweep(2)
            act.wait_ge(sweep_done[2], 1)

            def layer(i, b):
                if chunk_in(i, i):
                    after(act, l_product, i - 1)
                    act.nop(nofuse=True)
                    nc.scalar.copy(stage_t[:, b, :], sums[:, bass.ds(i * CW, CW)]).then_inc(l_staged, 1)
                if chunk_in(i, i - 2):
                    act.wait_ge(l_turned, i - 1)
                    after(act, l_out, i - 2)
                    nc.scalar.copy(hid_t[0:D, :], bank(2, CW)[0:D, :]).then_inc(l_copied, 1)
                if chunk_in(i, i - 1):
                    act.wait_ge(l_mean, i * 4)
                    nc.scalar.activation(stage_r[:, 1 - b, :], stage_r[:, 1 - b, :], ACT.Relu).then_inc(l_relu, 1)
            over_steps(act, layer)

        @block.tensor
        def _(pe):
            def scatter(k, visits_of_group, values, width):
                count, before = visits_of_group
                pe.nop(nofuse=True)
                with pe.Fori(0, count) as v:
                    pe.wait_ge(hit_built[k], before + v + 1)
                    pe.wait_ge(summed[k], before + v + 1)
                    pe.nop(nofuse=True)
                    for j in range(TILES):
                        mm = pe.matmul(bank(2, WINDOW)[0:width, :], values[:, j, 0:width], hit[:, j, :],
                                       start=(j == 0), stop=(j == TILES - 1))
                    mm.then_inc(scattered[k], 1)

            pe.wait_ge(pool_consts, 9)
            pe.wait_ge(consts, 2)

            pe.wait_ge(plan_c_step, 1)
            for q in range(TPS):
                mm = pe.transpose(psum[0:NS, q * P:(q + 1) * P], dst_t[:, q * NS:(q + 1) * NS], ident[:])
            mm.then_inc(tiles_turned, 1)
            pe.wait_ge(plan_c_step, 4)
            for q in range(0, TPS, 4):
                cols = min(4, TPS - q) * NS
                mm = pe.matmul(bank(q // 4, cols), ones[0:NS, :], first_t[0:NS, q * NS:q * NS + cols],
                               start=True, stop=True)
            mm.then_inc(firsts_spread, 1)

            pe.wait_ge(weights_loaded, 16 * 11)
            pe.transpose(bank(6)[0:D, 0:D + 1], w1b_b[:], ident[0:D + 1, 0:D + 1]).then_inc(weights_made, 1)
            pe.wait_ge(weights_step, 1)
            pe.matmul(bank(7)[0:D + 1, 0:D], w1b_t[:], w2a_m[:], start=True, stop=True).then_inc(weights_made, 1)

            pe.wait_ge(plan_ready, 1)
            for k in range(2):
                def sum_rows(g, n, r):
                    visits_of_group = group_plan(pe, g)[1:]
                    pe.wait_ge(gathered[k][r], GROUP_LANDED * (n + 1))
                    scatter(k, visits_of_group, ring[:, r], D)

                def place_group(g, n, r, sums_done):
                    pe.wait_ge(gathered[k][r], GROUP_LANDED * (n + 1))
                    pe.wait_ge(hit_built[k], g + 1)
                    pe.wait_ge(summed[k], sums_done)
                    pe.nop(nofuse=True)
                    for j in range(TILES):
                        mm = pe.matmul(bank(6, WINDOW)[0:D, :], ring[:, r, j, :], hit[:, j, :],
                                       start=(j == 0), stop=(j == TILES - 1))
                    mm.then_inc(scattered[k], 1)

                def place_supertile(s, sums_done):
                    pe.wait_ge(parts_ready[k], s * 2 + 2)
                    pe.wait_ge(summed[k], sums_done)
                    pe.nop(nofuse=True)
                    pe.matmul(bank(7, WIDE)[0:D, :], parts[:], hit_c[:], start=True, stop=True)\
                        .then_inc(placed[k], 1)

                def apply(s, b, a, z):
                    if a == 0:
                        tile_copied(pe, k, s, BY_VECTOR[-1])
                        tile_copied(pe, k, s, TPS - 1)
                        pe.nop(nofuse=True)
                    weights = counts[b].rearrange("p (s h) -> p s h", h=NT)
                    for c in range(a, z):
                        mm = pe.matmul(bank(4 + b, 3 * D), weights[:, :, c],
                                       thirds[:, c].rearrange("p a d -> p (a d)"),
                                       start=(c == 0), stop=(c == NT - 1))
                    if z == NT:
                        mm.then_inc(applied[k], 1)

                def supertile(s, b, n):
                    static = isinstance(s, int)
                    for t in range(TPS):
                        pe.wait_ge(marked[k], s * (2 * TPS) + 2 * t + 2)
                        if not static or s or t >= 2:
                            tile_copied(pe, k, s, t - 2)
                        pe.nop(nofuse=True)
                        slot = (b * TPS + t) % MARKS
                        for a in range(2):
                            mm = pe.matmul(bank(first_bank(b, t) + a, HK), low_ring[:, slot, :],
                                           key_ring[:, slot, a * HK:(a + 1) * HK], start=True, stop=True)
                        mm.then_inc(counted[k], 1)
                        if t >= 1 and not (static and s == 0):
                            apply(s - 1, 1 - b, NT * (t - 1) // (TPS - 1), NT * t // (TPS - 1))
                        if t == 3 and not (static and s < 2):
                            place_supertile(s - 2, sums_before(s) - 1)
                        if t == 8:
                            place_group(s * 2, n, 2 * b, sums_before(s) + (0 if static and s == 0 else 1))
                        if t == TPS - 1:
                            place_group(s * 2 + 1, n, 2 * b + 1,
                                        sums_before(s) + (1 if static and s == 0 else 2 if static else 3))

                def narrow():
                    pe.wait_ge(part_cast[k], 6)
                    pe.wait_ge(split_step[k], 7)
                    over_supertiles(pe, supertile)
                    total = sums_before(NS)
                    apply(NS - 1, 1, 0, NT)
                    place_supertile(NS - 2, total)
                    place_supertile(NS - 1, total + 2)
                    over_late_groups(pe, lambda g, n, r: place_group(g, n, r, g - 2 * NS + total + 3))
                either(pe, narrow, lambda: over_groups(pe, sum_rows))
                if k == 1:
                    break
                pe.sem_inc(sums_turned, 2)

                def turn(c, b):
                    pe.wait_ge(sums_staged, c + 1)
                    pe.wait_ge(sums_taken, c + 1)
                    pe.nop(nofuse=True)
                    for t in range(CHUNK):
                        mm = pe.transpose(bank(b)[:, t * D:(t + 1) * D], stage_t[0:D, b, t * P:(t + 1) * P],
                                          ident[0:D, 0:D])
                    mm.then_inc(sums_turned, 1)
                over_chunks(pe, turn)

            def turn_x(c, b):
                pe.wait_ge(m_staged, c + 1)
                if not isinstance(c, int) or c >= 2:
                    pe.wait_ge(m_centred, c * 4 - 7)
                pe.nop(nofuse=True)
                for t in range(CHUNK):
                    mm = pe.transpose(bank(b)[:, t * D:(t + 1) * D], stage_t[0:D, b, t * P:(t + 1) * P],
                                      ident[0:D, 0:D])
                mm.then_inc(m_turned, 1)

            def norm_and_project(i, b):
                if chunk_in(i, i + 1):
                    turn_x(i + 1, 1 - b)
                if chunk_in(i, i - 2):
                    pe.wait_ge(m_h_copied, i - 1)
                    after(pe, m_table, i - 2)
                    after(pe, m_hidden, i - 2)
                    pe.nop(nofuse=True)
                    for t in range(CHUNK):
                        mm = pe.matmul(projected()[:, t, :], h_t[:, t * P:(t + 1) * P], w_node[:],
                                       start=True, stop=True)
                    mm.then_inc(m_projected, 1)
                if chunk_in(i, i - 1):
                    pe.wait_ge(m_h, i * 2)
                    after(pe, m_h_copied, i - 1)
                    pe.nop(nofuse=True)
                    for t in range(CHUNK):
                        mm = pe.transpose(bank(2, CW)[0:D, t * P:(t + 1) * P],
                                          stage_r[:, 1 - b, t * D:(t + 1) * D], ident[:])
                    mm.then_inc(m_h_turned, 1)
            pe.wait_ge(sweep_done[1], 1)
            pe.wait_ge(late_consts, 1)
            turn_x(0, 0)
            over_steps(pe, norm_and_project)

            pe.wait_ge(late_consts, 2)
            pe.sem_inc(multiplied, RING)

            def messages(g, n, r):
                visits_of_group = group_plan(pe, g)[1:]
                pe.wait_ge(attr_loaded[r], 16 * (n + 1))
                pe.wait_ge(slot_free[2], g + 1)
                for j in range(TILES // 2):
                    mm = pe.matmul(bank(r % 2)[:, j * P:(j + 1) * P],
                                   attr_ring[:, r, j * TILE:(j + 1) * TILE], w_attr[:], start=True, stop=True)
                mm.then_inc(multiplied, 1)
                pe.wait_ge(msg_ready, g + 3)
                scatter(2, visits_of_group, msg[:, r % 2], D + 1)
            over_groups(pe, messages)

            pe.wait_ge(sweep_done[2], 1)

            def layer(i, b):
                if chunk_in(i, i):
                    pe.wait_ge(l_staged, i + 1)
                    if not isinstance(i, int) or i >= 2:
                        pe.wait_ge(l_mean, i * 4 - 5)
                    pe.nop(nofuse=True)
                    for t in range(CHUNK):
                        mm = pe.matmul(bank(b)[:, t * (D + 1):(t + 1) * (D + 1)],
                                       stage_t[:, b, t * P:(t + 1) * P], w_sums[:], start=True, stop=True)
                    mm.then_inc(l_product, 1)
                if chunk_in(i, i - 2):
                    pe.wait_ge(l_copied, i - 1)
                    if isinstance(i, int):
                        after(pe, l_rows, i - 3)
                    else:
                        pe.wait_ge(l_mean, i * 4)
                    pe.nop(nofuse=True)
                    for t in range(CHUNK):
                        mm = pe.matmul(bank(4 + b)[:, t * D:(t + 1) * D], hid_t[:, t * P:(t + 1) * P], w2b_b[:],
                                       start=True, stop=True)
                    mm.then_inc(l_out, 1)
                if chunk_in(i, i - 1):
                    pe.wait_ge(l_relu, i)
                    after(pe, l_copied, i - 1)
                    pe.nop(nofuse=True)
                    for t in range(CHUNK):
                        mm = pe.transpose(bank(2, CW)[0:D, t * P:(t + 1) * P],
                                          stage_r[:, 1 - b, t * D:(t + 1) * D], ident[:])
                    mm.then_inc(l_turned, 1)
            over_steps(pe, layer)

        @block.vector
        def _(dve):
            def norm():
                def spread(col):
                    return col.unsqueeze(2).to_broadcast([P, NT // 2, D])

                for h in range(2):
                    dve.wait_ge(x_loaded[h], 16)
                    nc.vector.tensor_reduce(half(col_a, h), half(x_rows, h), AX.X, ALU.add).then_inc(norm_step, 1)
                    dve.wait_ge(norm_step, h * 3 + 1)
                    nc.vector.tensor_scalar(half(col_b, h), half(col_a, h), 1.0 / D, None, ALU.mult)\
                        .then_inc(norm_step, 1)
                    dve.wait_ge(norm_step, h * 3 + 2)
                    nc.vector.tensor_tensor(half(rows_work, h), half(x_rows, h), spread(half(col_b, h)),
                                            ALU.subtract).then_inc(norm_step, 1)
                for h in range(2):
                    dve.wait_ge(squared, h + 1)
                    nc.vector.tensor_reduce(half(col_a, h), half(rows, h), AX.X, ALU.add).then_inc(norm_step, 1)
                for h in range(2):
                    dve.wait_ge(deviation_ready, h + 1)
                    nc.vector.reciprocal(half(col_a, h), half(col_b, h)).then_inc(inverted, 1)
                    dve.wait_ge(inverted, h + 1)
                    nc.vector.scalar_tensor_tensor(out=half(rows, h), in0=half(rows_work, h), scalar=0.0,
                                                   in1=spread(half(col_a, h)), op0=ALU.max, op1=ALU.mult)\
                        .then_inc(norm_step, 1)

            nc.vector.memset(w_attr[:], 0.0).then_inc(consts, 1)
            nc.vector.memset(eps[:], EPS)
            nc.vector.memset(w_sums[0:D, D:D + 1], 0.0)
            nc.vector.memset(w_sums[D:D + 1, D:D + 1], 1.0)
            nc.vector.memset(limits[:, 0], 0.0)
            nc.vector.memset(ones[:], 1.0).then_inc(consts, 1)

            dst_3 = dst_i.rearrange("p (g t) -> p g t", t=TILES)
            dve.wait_ge(dst_loaded, 16)
            nc.vector.tensor_reduce(span[:, 0:NG], dst_3, AX.X, ALU.max).then_inc(plan_step, 1)
            nc.vector.tensor_reduce(windows, dst_3, AX.X, ALU.min).then_inc(plan_step, 1)
            dve.wait_ge(plan_step, 2)
            nc.vector.tensor_scalar(span[:, NG:2 * NG], windows, -1.0, None, ALU.mult).then_inc(plan_step, 1)

            dve.wait_ge(dst_c_loaded, 16)
            nc.vector.tensor_copy(dst_t, dst_t.bitcast(I32)).then_inc(plan_c_step, 1)
            dve.wait_ge(tiles_turned, 1)
            turned = psum[0:NS, 0:TPS * P].rearrange("p (q e) -> p q e", e=P)
            nc.vector.tensor_reduce(col_min[0:NS, :], turned, AX.X, ALU.min).then_inc(plan_c_step, 1)
            nc.vector.tensor_reduce(col_max[0:NS, :], turned, AX.X, ALU.max).then_inc(plan_c_step, 1)
            dve.wait_ge(plan_c_step, 3)
            nc.vector.tensor_tensor(first_t[0:NS, :].rearrange("p (q m) -> p q m", q=TPS),
                                    ident[0:NS, 0:NS].unsqueeze(1).to_broadcast([NS, TPS, NS]),
                                    col_min[0:NS, :].unsqueeze(2).to_broadcast([NS, TPS, NS]), ALU.mult)\
                .then_inc(plan_c_step, 1)
            nc.vector.tensor_tensor(col_max[0:NS, :], col_max[0:NS, :], col_min[0:NS, :], ALU.subtract)\
                .then_inc(plan_c_step, 1)
            dve.wait_ge(plan_c_step, 5)
            nc.vector.tensor_reduce(limits[0:NS, 0, 0:1], col_max[0:NS, :], AX.X, ALU.max).then_inc(plan_c_step, 1)
            dve.wait_ge(pool_consts, 9)
            nc.vector.tensor_tensor(col_b[:, 0:TPS], mask[:], number[:, 0:TPS], ALU.mult).then_inc(plan_c_step, 1)
            dve.wait_ge(plan_c_step, 7)
            nc.vector.tensor_reduce(part_no[:], col_b[:, 0:TPS], AX.X, ALU.add).then_inc(plan_c_step, 1)
            dve.wait_ge(plan_c_step, 8)
            nc.vector.tensor_scalar(part_no[:], part_no[:], -float(SPAN), None, ALU.mult).then_inc(plan_c_step, 1)
            dve.wait_ge(plan_c_step, 9)
            nc.vector.tensor_tensor(part_no[:], part_no[:], tick_i[:], ALU.add).then_inc(plan_c_step, 1)
            dve.wait_ge(firsts_spread, 1)
            dve.wait_ge(plan_c_step, 10)
            for q in range(0, TPS, 4):
                cols = min(4, TPS - q) * NS
                nc.vector.tensor_copy(first_t[:, q * NS:q * NS + cols], bank(q // 4, cols))\
                    .then_inc(plan_c_step, 1)
            at = 10 + -(-TPS // 4)

            norm()

            dve.wait_ge(plan_c_step, at)
            nc.vector.tensor_tensor(dst_t, dst_t, first_t, ALU.subtract).then_inc(plan_c_step, 1)
            dve.wait_ge(src_c_loaded, 16)
            keys_low, keys_high = keys[:, 0:NS, 0, :], keys[:, 0:NS, 1, :]
            nc.vector.tensor_scalar(work[:, 0:NC].bitcast(I32), src_t, P - 1, None, ALU.bitwise_and)\
                .then_inc(plan_c_step, 1)
            nc.vector.tensor_scalar(src_t, src_t, P.bit_length() - 1, None, ALU.logical_shift_right)\
                .then_inc(plan_c_step, 1)
            dve.wait_ge(plan_c_step, at + 3)
            nc.vector.tensor_copy(keys_low, work[:, 0:NC].bitcast(I32).rearrange("p (s t) -> p s t", t=TPS))\
                .then_inc(plan_c_step, 1)
            nc.vector.scalar_tensor_tensor(out=keys_high, in0=dst_t.rearrange("p (s t) -> p s t", t=TPS),
                                           scalar=float(NT), in1=src_t.rearrange("p (s t) -> p s t", t=TPS),
                                           op0=ALU.mult, op1=ALU.add).then_inc(plan_c_step, 1)
            firsts = first_t.rearrange("p (s t) -> p s t", t=TPS)
            nc.vector.tensor_tensor(work[:, NC:2 * NC].rearrange("p (s t) -> p s t", t=TPS), firsts,
                                    mask[:].unsqueeze(1).to_broadcast([P, NS, TPS]), ALU.mult)\
                .then_inc(plan_c_step, 1)
            nc.vector.tensor_copy(plan_c[0:1, :], firsts[0:1, :, 0]).then_inc(plan_c_step, 1)
            dve.wait_ge(plan_c_step, at + 7)
            nc.vector.tensor_reduce(slot_node[:], work[:, NC:2 * NC].rearrange("p (s t) -> p s t", t=TPS),
                                    AX.X, ALU.add).then_inc(plan_c_step, 1)
            dve.wait_ge(plan_c_step, at + 8)
            nc.vector.tensor_tensor(slot_node[:], slot_node[:], firsts[:, :, 0], ALU.subtract)\
                .then_inc(plan_c_step, 1)
            dve.wait_ge(plan_c_step, at + 9)
            nc.vector.tensor_scalar(slot_node[:], slot_node[:], part_no[:, 0:1], None, ALU.add)\
                .then_inc(plan_c_step, 1)
            dve.wait_ge(plan_c_step, at + 10)
            slots = TPS * SPAN
            nc.vector.tensor_reduce(limits[0:slots, 0, 1:2], slot_node[0:slots, :], AX.X, ALU.max)\
                .then_inc(plan_c_step, 1)
            nc.vector.tensor_reduce(limits[0:slots, 0, 2:3], slot_node[0:slots, :], AX.X, ALU.min)\
                .then_inc(plan_c_step, 1)
            dve.wait_ge(plan_c_step, at + 12)
            nc.vector.tensor_scalar(limits[0:slots, 0, 2:3], limits[0:slots, 0, 2:3], -1.0, None, ALU.mult)\
                .then_inc(plan_c_step, 1)

            dve.wait_ge(spans_reduced, 1)
            nc.vector.tensor_tensor(dst_rel[:], dst_3, minus_first.unsqueeze(2).to_broadcast([P, NG, TILES]),
                                    ALU.add).then_inc(plan_step, 1)
            nc.vector.tensor_tensor(windows_i, last, minus_first, ALU.add).then_inc(plan_step, 1)
            dve.wait_ge(plan_step, 5)
            nc.vector.tensor_scalar(windows_i, windows_i, SHIFT, None, ALU.logical_shift_right)\
                .then_inc(plan_step, 1)
            dve.wait_ge(plan_step, 6)
            nc.vector.tensor_scalar(windows, windows_i, 1.0, None, ALU.add).then_inc(plan_step, 1)
            dve.wait_ge(plan_step, 7)
            nc.vector.tensor_reduce(limits[:, 0, 3:4], windows[:, 0:GATHERED], AX.X, ALU.max)\
                .then_inc(plan_c_step, 1)
            nc.vector.memset(span[:, 0:NG], 1.0).then_inc(plan_step, 1)
            dve.wait_ge(plan_step, 8)
            nc.vector.tensor_tensor_scan(visits, span[:, 0:NG], windows, 0.0, ALU.mult, ALU.add)\
                .then_inc(plan_step, 1)
            dve.wait_ge(plan_step, 9)
            nc.vector.tensor_tensor(plan[0:1, :, 2], visits[0:1, :], windows[0:1, :], ALU.subtract)
            nc.vector.tensor_copy(plan[0:1, :, 1], windows[0:1, :])
            nc.vector.tensor_scalar(plan[0:1, :, 0], minus_first[0:1, :], -1.0, None, ALU.mult)\
                .then_inc(plan_step, 1)
            dve.wait_ge(limits_reduced, 1)
            for i, most in enumerate((SPAN - 1, WIDE - 1, 0, 1)):
                nc.vector.tensor_scalar(limits[:, 0, i:i + 1], limits[:, 1, i:i + 1], float(most), None,
                                        ALU.is_gt).then_inc(plan_step, 1)
            dve.wait_ge(plan_step, 14)
            nc.vector.tensor_reduce(wide[:], limits[:, 0, :], AX.X, ALU.max).then_inc(plan_step, 1)
            dve.wait_ge(plan_step, 15)
            dve.wait_ge(pool_consts, 9)
            nc.vector.memset(tick[:, 4:5], 0.0).then_inc(plan_ready, 1)

            def split(k):
                step = split_step[k]
                for part in range(2):
                    for h in range(2):
                        dve.wait_ge(part_cast[k], part * 2 + h + 1)
                        if part:
                            dve.wait_ge(step, h + 1)
                        nc.vector.tensor_tensor(half(rows_work, h), half(rows if part == 0 else rows_work, h),
                                                half(thirds, h)[:, :, part, :], ALU.subtract).then_inc(step, 1)
                nc.vector.memset(arena[:, NT * D:], 0.0).then_inc(step, 1)
                dve.wait_ge(table_stored[k], 16 * STORES[k])
                for b in range(2):
                    nc.vector.memset(counts[b][:, TPS * KEYS:P * NT], 0.0).then_inc(step, 1)
                dve.wait_ge(part_cast[k], 6)
                dve.wait_ge(step, 7)

            def sweep(k):
                width = D if k < 2 else D + 1
                zeroed = work if k < 2 else arena[:]
                nc.vector.memset(zeroed, 0.0).then_inc(summed[k], 1)
                dve.sem_inc(slot_free[k], 2)
                dve.sem_inc(rel_step[k], 1)
                if k == 2:
                    dve.sem_inc(msg_used, 2)

                def window_at(begin, size):
                    begin = nc.s_assert_within(begin, 0, COLS - size,
                                               skip_runtime_bounds_check_because="spans end within the nodes")
                    return sums[0:width, bass.ds(begin, size)]

                def mark_hits(rel):
                    nc.vector.tensor_tensor(
                        hit[:], number[:, 0:WINDOW].unsqueeze(1).to_broadcast([P, TILES, WINDOW]),
                        rel.unsqueeze(2).to_broadcast([P, TILES, WINDOW]), ALU.is_equal).then_inc(hit_built[k], 1)

                def body(g, n, r):
                    first, count, before = group_plan(dve, g)
                    if k == 2:
                        dve.wait_ge(multiplied, g + 1 + RING)
                        dve.wait_ge(gathered[2][r], GROUP_LANDED * (n + 1))
                        dve.wait_ge(msg_ready, g + 1)
                        nc.vector.tensor_tensor(pre[:, r % 2, :], bank(r % 2),
                                                ring[:, r].rearrange("p t d -> p (t d)"), ALU.add)\
                            .then_inc(slot_free[2], 1)
                    dve.wait_ge(rel_step[k], before + g + 1)
                    dve.nop(nofuse=True)
                    nc.vector.tensor_copy(rel_now[:], dst_rel[:, bass.ds(g, 1), :].rearrange("p g t -> p (g t)"))\
                        .then_inc(rel_step[k], 1)
                    with dve.Fori(0, count) as v:
                        dve.wait_ge(rel_step[k], before + g + v + 2)
                        mark_hits(rel_now[:])
                        dve.wait_ge(hit_built[k], before + v + 1)
                        nc.vector.tensor_scalar(rel_now[:], rel_now[:], -float(WINDOW), None, ALU.add)\
                            .then_inc(rel_step[k], 1)
                        window = window_at(first + v * WINDOW, WINDOW)
                        dve.wait_ge(scattered[k], before + v + 1)
                        dve.wait_ge(summed[k], before + v + 1)
                        dve.nop(nofuse=True)
                        nc.vector.tensor_tensor(window, window, bank(2, WINDOW)[0:width, :], ALU.add)\
                            .then_inc(summed[k], 1)
                    nc.vector.memset(tick[:, 0:1], 0.0).then_inc(slot_free[k] if k < 2 else msg_used, 1)

                def mark_group(g):
                    mark_hits(dst_rel[:, bass.ds(g, 1), :].rearrange("p g t -> p (g t)"))

                def sum_group(g, sums_done):
                    first = dve.value_load(plan[0:1, bass.ds(g, 1), 0:1], min_val=0, max_val=n_nodes)
                    window = window_at(first, WINDOW)
                    dve.wait_ge(scattered[k], g + 1)
                    dve.wait_ge(summed[k], sums_done)
                    dve.nop(nofuse=True)
                    nc.vector.tensor_tensor(window, window, bank(6, WINDOW)[0:D, :], ALU.add)\
                        .then_inc(summed[k], 1)

                def add_parts(s, b):
                    dve.wait_ge(applied[k], s + 1)
                    dve.nop(nofuse=True)
                    nc.vector.tensor_reduce(parts[:], bank(4 + b, 3 * D).rearrange("p (a d) -> p d a", a=3),
                                            AX.X, ALU.add).then_inc(parts_ready[k], 1)
                    nc.vector.tensor_scalar(hit_c[:], number[:, 0:WIDE], slot_node[:, bass.ds(s, 1)], None,
                                            ALU.is_equal).then_inc(parts_ready[k], 1)

                def sum_supertile(s, sums_done):
                    first = dve.value_load(plan_c[0:1, bass.ds(s, 1)], min_val=0, max_val=n_nodes)
                    window = window_at(first, WIDE)
                    dve.wait_ge(placed[k], s + 1)
                    dve.wait_ge(summed[k], sums_done)
                    dve.nop(nofuse=True)
                    nc.vector.tensor_tensor(window, window, bank(7, WIDE)[0:D, :], ALU.add)\
                        .then_inc(summed[k], 1)

                def supertile(s, b, n):
                    static = isinstance(s, int)
                    dve.wait_ge(keys_staged[k], s + 1)
                    done = sums_before(s)
                    for t in range(TPS):
                        slot = (b * TPS + t) % MARKS
                        if not static or s or t >= MARKS:
                            dve.wait_ge(counted[k], s * TPS + (t - MARKS + 1))
                        nc.vector.tensor_scalar(low_ring[:, slot, :], number[:, 0:P], keys_now[:, b, 0, t:t + 1],
                                                None, ALU.is_equal).then_inc(marked[k], 1)
                        nc.vector.tensor_scalar(key_ring[:, slot, :], number[:], keys_now[:, b, 1, t:t + 1],
                                                None, ALU.is_equal).then_inc(marked[k], 1)
                        u = t - LAG
                        if u in BY_VECTOR:
                            if u == BY_VECTOR[0] and not (static and s < 2):
                                dve.wait_ge(applied[k], s - 1)
                            dve.wait_ge(counted[k], s * TPS + u + 1)
                            nc.vector.tensor_copy(slot_counts(b, u), tile_counts(b, u)).then_inc(copied_v[k], 1)
                        if t == 1 and not (static and s < 2):
                            add_parts(s - 2, b)
                        if t == 2 and not (static and s == 0):
                            sum_group(s * 2 - 1, done)
                            done = done + 1
                        if t == 4:
                            mark_group(s * 2)
                        if t == 7 and not (static and s < 2):
                            sum_supertile(s - 2, done)
                            done = done + 1
                        if t == 11:
                            sum_group(s * 2, done)
                            done = done + 1
                        if t == 13:
                            mark_group(s * 2 + 1)

                def late_group(g, n, r):
                    mark_group(g)
                    sum_group(g, g - 2 * NS + sums_before(NS) + 3)

                def narrow():
                    dve.sem_inc(copied_a[k], 1)
                    dve.sem_inc(copied_v[k], 1)
                    over_supertiles(dve, supertile)
                    total = sums_before(NS)
                    sum_group(2 * NS - 1, total)
                    add_parts(NS - 2, 0)
                    sum_supertile(NS - 2, total + 1)
                    add_parts(NS - 1, 1)
                    sum_supertile(NS - 1, total + 2)
                    over_late_groups(dve, late_group)

                if k < 2:
                    either(dve, narrow, lambda: over_groups(dve, body))
                else:
                    over_groups(dve, body)
                nc.vector.memset(tick[:, 1 + k:2 + k], 0.0).then_inc(sweep_done[k], 1)

            dve.wait_ge(weights_made, 1)
            nc.vector.tensor_copy(w1b_t[:], bank(6)[0:D, 0:D + 1]).then_inc(weights_step, 1)
            dve.wait_ge(weights_made, 2)
            nc.vector.tensor_copy(w_sums[:, 0:D], bank(7)[0:D + 1, 0:D]).then_inc(weights_step, 1)

            split(0)
            sweep(0)
            dve.sem_inc(sums_taken, 2)

            def take(c, b):
                dve.wait_ge(sums_turned, c + 3)
                dve.nop(nofuse=True)
                nc.vector.tensor_copy(rows_at(rows, c), bank(b, RW).rearrange("p (t d) -> p t d", d=D))\
                    .then_inc(sums_taken, 1)
            over_chunks(dve, take)
            dve.wait_ge(sums_staged, NCH)
            dve.wait_ge(sums_taken, NCH + 2)
            split(1)
            sweep(1)
            nc.vector.memset(h_t[D:D + 1, :], 1.0).then_inc(late_consts, 1)

            def norm_and_project(i, b):
                def spread(col):
                    return col.unsqueeze(2).to_broadcast([P, CHUNK, D])

                if chunk_in(i, i - 1):
                    dve.wait_ge(m_squared, i)
                    nc.vector.tensor_reduce(col_n[:, 1 - b, 2, :], squares[1 - b], AX.X, ALU.add)\
                        .then_inc(m_summed, 1)
                if chunk_in(i, i):
                    x_now = rows_at(x_rows, i)
                    dve.wait_ge(x_again[b], (i - b) * 8 + 16)
                    dve.wait_ge(m_turned, i + 1)
                    dve.nop(nofuse=True)
                    nc.vector.tensor_tensor(x_now, x_now, bank(b, RW).rearrange("p (t d) -> p t d", d=D),
                                            ALU.add).then_inc(m_centred, 1)
                    dve.wait_ge(m_centred, i * 4 + 1)
                    dve.nop(nofuse=True)
                    nc.vector.tensor_reduce(col_n[:, b, 0, :], x_now, AX.X, ALU.add).then_inc(m_centred, 1)
                    dve.wait_ge(m_centred, i * 4 + 2)
                    nc.vector.tensor_scalar(col_n[:, b, 1, :], col_n[:, b, 0, :], 1.0 / D, None, ALU.mult)\
                        .then_inc(m_centred, 1)
                    dve.wait_ge(m_centred, i * 4 + 3)
                    dve.nop(nofuse=True)
                    nc.vector.tensor_tensor(centred[b], x_now, spread(col_n[:, b, 1, :]), ALU.subtract)\
                        .then_inc(m_centred, 1)
                if chunk_in(i, i - 1):
                    dve.wait_ge(m_deviation, i)
                    nc.vector.reciprocal(col_n[:, 1 - b, 3, :], col_n[:, 1 - b, 3, :]).then_inc(m_h, 1)
                    dve.wait_ge(m_h, i * 2 - 1)
                    nc.vector.scalar_tensor_tensor(
                        out=stage_r[:, 1 - b, :].rearrange("p (t d) -> p t d", d=D), in0=centred[1 - b],
                        scalar=0.0, in1=spread(col_n[:, 1 - b, 3, :]), op0=ALU.max, op1=ALU.mult)\
                        .then_inc(m_h, 1)
                if chunk_in(i, i - 2):
                    dve.wait_ge(m_projected, i - 1)
                    dve.wait_ge(m_table, i - 1)
                    dve.nop(nofuse=True)
                    nc.vector.tensor_copy(rows_at(rows, i - 2), projected()[:, :, D:2 * D]).then_inc(m_hidden, 1)
            over_steps(dve, norm_and_project)
            dve.wait_ge(table_stored[2], 16 * NCH)
            nc.vector.memset(msg[:, :, :, D:D + 1], 1.0).then_inc(late_consts, 1)
            sweep(2)

            def layer(i, b):
                if chunk_in(i, i):
                    product = bank(b, CHUNK * (D + 1)).rearrange("p (t d) -> p t d", d=D + 1)
                    here = stage_r[:, b, :].rearrange("p (t d) -> p t d", d=D)
                    dve.wait_ge(l_product, i + 1)
                    if not isinstance(i, int) or i >= 2:
                        dve.wait_ge(l_turned, i - 1)
                    dve.nop(nofuse=True)
                    nc.vector.tensor_scalar(col_n[:, b, 0, :], product[:, :, D], 1.0, None, ALU.max)\
                        .then_inc(l_mean, 1)
                    dve.wait_ge(l_mean, i * 4 + 1)
                    nc.vector.reciprocal(col_n[:, b, 1, :], col_n[:, b, 0, :]).then_inc(l_mean, 1)
                    dve.wait_ge(l_mean, i * 4 + 2)
                    nc.vector.tensor_tensor(here, product[:, :, 0:D],
                                            col_n[:, b, 1, :].unsqueeze(2).to_broadcast([P, CHUNK, D]),
                                            ALU.mult).then_inc(l_mean, 1)
                    dve.wait_ge(l_mean, i * 4 + 3)
                    dve.nop(nofuse=True)
                    nc.vector.tensor_tensor(here, here, rows_at(rows, i), ALU.add).then_inc(l_mean, 1)
                if chunk_in(i, i - 2):
                    dve.wait_ge(l_out, i - 1)
                    dve.nop(nofuse=True)
                    nc.vector.tensor_tensor(rows_at(rows, i - 2), bank(4 + b, RW).rearrange("p (t d) -> p t d", d=D),
                                            rows_at(x_rows, i - 2), ALU.add).then_inc(l_rows, 1)
            over_steps(dve, layer)


def kernel(x, src, dst, edge_attr_64, L1_gnn_u, L1_gnn_w1a, L1_gnn_b1a, L1_gnn_w1b, L1_gnn_b1b,
           L1_gnn_w2a, L1_gnn_b2a, L1_gnn_w2b, L1_gnn_b2b):
    import numpy as _np
    import concourse.bacc as _bacc
    from concourse import mybir as _mybir
    from concourse.bass_utils import run_bass_kernel_spmd as _run

    n_nodes, d = x.shape
    n_edges = src.shape[0]
    node_rows = -(-n_nodes // (P * CHUNK)) * P * CHUNK
    groups = -(-n_edges // (TILE * TILES))
    n_pad = groups * TILE * TILES - n_edges

    def by_partition(index, fill):
        a = _np.concatenate([_np.asarray(index), _np.full(n_pad, fill, _np.asarray(index).dtype)])
        return _np.ascontiguousarray(a.reshape(groups, TILE, TILES).transpose(1, 0, 2).reshape(TILE, -1))

    def by_tile(index, fill):
        a = _np.asarray(index)[GATHERED * TILES * TILE:]
        a = _np.concatenate([a, _np.full(-len(a) % (2 * TPS * TILE), fill, a.dtype)])
        return _np.ascontiguousarray(a.reshape(-1, TILE).T)

    attr = _np.concatenate([_np.asarray(edge_attr_64), _np.zeros((n_pad, d), _np.float32)])
    attr = attr.reshape(groups, TILE, TILES // 2, 2, d).transpose(0, 3, 4, 2, 1)
    arrays = {
        "x": _np.concatenate([_np.asarray(x), _np.zeros((node_rows - n_nodes, d), _np.float32)]),
        "src": by_partition(src, 0),
        "dst": by_partition(dst, n_nodes),
        "src_c": by_tile(src, 0),
        "dst_c": by_tile(dst, n_nodes),
        "attr": _np.ascontiguousarray(attr.reshape(groups, 2 * d, TILES // 2 * TILE)),
        "w1a": L1_gnn_w1a, "b1a": L1_gnn_b1a, "w1b": L1_gnn_w1b, "b1b": L1_gnn_b1b,
        "w2a": L1_gnn_w2a, "b2a": L1_gnn_b2a, "w2b": L1_gnn_w2b, "b2b": L1_gnn_b2b,
    }
    arrays = {n: _np.ascontiguousarray(a) for n, a in arrays.items()}
    nc = _bacc.Bacc("TRN2", target_bir_lowering=False, num_devices=1)
    args = [nc.dram_tensor(f"in_{n}", a.shape, _mybir.dt.from_np(a.dtype), kind="ExternalInput").ap()
            for n, a in arrays.items()]
    out = nc.dram_tensor("out_0", (n_nodes, d), _mybir.dt.float32, kind="ExternalOutput").ap()
    gnn_kernel(nc, *args, out)
    r = _run(nc, [{f"in_{n}": a for n, a in arrays.items()}], core_ids=[0])
    return r.results[0]["out_0"]
```
